# Optimizing a Trainium2 kernel written in Bass

```python
import numpy as np
import jax
import jax.numpy as jnp

def _softmax(x, axis=-1):
    return jax.nn.softmax(x, axis=axis)

def _gelu(x):
    return jax.nn.gelu(x, approximate=True)

def _silu(x):
    return jax.nn.silu(x)

def _sigmoid(x):
    return jax.nn.sigmoid(x)

def _layernorm(x, axis=-1, eps=1e-05):
    m = jnp.mean(x, axis=axis, keepdims=True)
    v = jnp.var(x, axis=axis, keepdims=True)
    return (x - m) / jnp.sqrt(v + eps)

def _scatter_add(tgt, idx, src, axis=0):
    return tgt.at[idx].add(src)

def _segment_sum(src, seg, n):
    return jax.ops.segment_sum(src, seg, n)
kernel_name = 'mk_gnn_resnorm_d4_gnn_r64_7ea0d1'

def setup_inputs(seed: int=0):
    np.random.seed(seed)
    _w = jnp.asarray

    def _rec_inputs():
        import jax
        import jax.numpy as jnp
        _gk = jax.random.key(seed)
        x = -0.000202 + 1 * jax.random.normal(jax.random.fold_in(_gk, 1), (100000, 128), jnp.float32)
        src = jax.random.randint(jax.random.fold_in(_gk, 2), (25000,), 0, 100000, jnp.int32)
        dst = jax.random.randint(jax.random.fold_in(_gk, 3), (25000,), 0, 100000, jnp.int32)
        _o = jnp.argsort(dst, stable=True)
        src = src[_o]
        dst = dst[_o]
        edge_attr3_10x16 = -6.74381e-05 + 0.999835 * jax.random.normal(jax.random.fold_in(_gk, 12), (25000, 10, 16), jnp.float32)
        edge_weight = jax.random.uniform(jax.random.fold_in(_gk, 14), (25000,), jnp.float32, 0.0, 1)
        return (x, src, dst, edge_attr3_10x16, edge_weight)
    x, src, dst, edge_attr3_10x16, edge_weight = _rec_inputs()

    def _L0_gnn_setup():
        import jax, jax.numpy as jnp
        import numpy as np
        LOG2 = 0.6931471805599453
        N_NODES = 50000
        N_EDGES = 500000
        NUM_HEADS = 10
        NUM_FILTERS = 16
        HIDDEN = 128
        key = jax.random.key(seed)
        ks = jax.random.split(key, 6)
        v = jax.random.normal(ks[0], (N_NODES, HIDDEN), dtype=jnp.float32)
        e = jax.random.normal(ks[1], (N_EDGES, NUM_HEADS, NUM_FILTERS), dtype=jnp.float32)
        edge_index = jax.random.randint(ks[2], (2, N_EDGES), 0, N_NODES, dtype=jnp.int64)
        d_in = NUM_HEADS * NUM_FILTERS
        W1 = jax.random.normal(ks[3], (HIDDEN, d_in), dtype=jnp.float32) * (1.0 / np.sqrt(d_in))
        b1 = jnp.zeros((HIDDEN,), dtype=jnp.float32)
        W2 = jax.random.normal(ks[4], (HIDDEN, HIDDEN), dtype=jnp.float32) * (1.0 / np.sqrt(HIDDEN))
        b2 = jnp.zeros((HIDDEN,), dtype=jnp.float32)
        return {'v': v, 'e': e, 'edge_index': edge_index, 'W1': W1, 'b1': b1, 'W2': W2, 'b2': b2}
    _L0_gnn_all = _L0_gnn_setup()
    _L0_gnn_in = {k: v for k, v in _L0_gnn_all.items() if k in ('W1', 'b1', 'W2', 'b2')}
    del _L0_gnn_all

    def _L1_gnn_setup():
        import jax, jax.numpy as jnp
        import numpy as np
        N_NODES = 50000
        N_EDGES = 12500
        D_IN = 128
        D_OUT = 128
        key = jax.random.key(seed)
        k = jax.random.split(key, 6)
        feat = jax.random.normal(k[0], (N_NODES, D_IN), dtype=jnp.float32)
        edge_weight = jax.random.uniform(k[1], (N_EDGES,), dtype=jnp.float32)
        src_idx = jax.random.randint(k[2], (N_EDGES,), 0, N_NODES, dtype=jnp.int32)
        dst_idx = jax.random.randint(k[3], (N_EDGES,), 0, N_NODES, dtype=jnp.int32)
        gain = float(np.sqrt(2.0))
        bound = gain * float(np.sqrt(6.0 / (D_IN + D_OUT)))
        W_self = jax.random.uniform(k[4], (D_OUT, D_IN), dtype=jnp.float32, minval=-bound, maxval=bound)
        W_neigh = jax.random.uniform(k[5], (D_OUT, D_IN), dtype=jnp.float32, minval=-bound, maxval=bound)
        b_self = jnp.zeros((D_OUT,), dtype=jnp.float32)
        b_neigh = jnp.zeros((D_OUT,), dtype=jnp.float32)
        return {'feat': feat, 'edge_weight': edge_weight, 'src_idx': src_idx, 'dst_idx': dst_idx, 'W_self': W_self, 'b_self': b_self, 'W_neigh': W_neigh, 'b_neigh': b_neigh}
    _L1_gnn_all = _L1_gnn_setup()
    _L1_gnn_in = {k: v for k, v in _L1_gnn_all.items() if k in ('W_self', 'b_self', 'W_neigh', 'b_neigh')}
    del _L1_gnn_all

    def _L2_gnn_setup():
        import jax, jax.numpy as jnp
        import numpy as np
        N_NODES = 100000
        N_EDGES = 25000
        F_IN = 128
        F_OUT = 128
        key = jax.random.key(seed)
        k1, k2, k3, k4, k5 = jax.random.split(key, 5)
        features = jax.random.normal(k1, (N_NODES, F_IN), dtype=jnp.float32)
        scale = float(np.sqrt(2.0 / (F_IN + F_OUT)))
        w_s = jax.random.normal(k2, (F_IN, F_OUT), dtype=jnp.float32) * scale
        w_n = jax.random.normal(k3, (F_IN, F_OUT), dtype=jnp.float32) * scale
        src = jax.random.randint(k4, (N_EDGES,), 0, N_NODES, dtype=jnp.int32)
        dst = jax.random.randint(k5, (N_EDGES,), 0, N_NODES, dtype=jnp.int32)
        return {'features': features, 'w_s': w_s, 'w_n': w_n, 'src': src, 'dst': dst}
    _L2_gnn_all = _L2_gnn_setup()
    _L2_gnn_in = {k: v for k, v in _L2_gnn_all.items() if k in ('w_s', 'w_n')}
    del _L2_gnn_all

    def _L3_gnn_setup():
        import jax, jax.numpy as jnp
        import numpy as np
        N_NODES = 30000
        IN_CH = 128
        HID_CH = 256
        K = 3
        N_EDGES = 7500

        def _norm_weights(edge_index, n):
            src, dst = (edge_index[0], edge_index[1])
            mask = src != dst
            ones = jnp.where(mask, 1.0, 0.0)
            deg = jax.ops.segment_sum(ones, src, num_segments=n)
            dis = jnp.where(deg > 0, deg ** (-0.5), 0.0)
            w = jnp.where(mask, -dis[src] * dis[dst], 0.0)
            return (src, dst, w)

        def _cheb_conv(x, src, dst, w, W, b, n):

            def lap(h):
                return jax.ops.segment_sum(w[:, None] * h[src], dst, num_segments=n)
            Tx_prev = x
            out = x @ W[0]
            if W.shape[0] > 1:
                Tx_cur = lap(x)
                out = out + Tx_cur @ W[1]
                for k in range(2, W.shape[0]):
                    Tx_next = 2.0 * lap(Tx_cur) - Tx_prev
                    out = out + Tx_next @ W[k]
                    Tx_prev, Tx_cur = (Tx_cur, Tx_next)
            return out + b
        key = jax.random.key(seed)
        k1, k2, k3, k4, k5, k6 = jax.random.split(key, 6)
        x = jax.random.normal(k1, (N_NODES, IN_CH), dtype=jnp.float32)
        edge_index = jax.random.randint(k2, (2, N_EDGES), 0, N_NODES, dtype=jnp.int64)
        s1 = (1.0 / (IN_CH * K)) ** 0.5
        s2 = (1.0 / (HID_CH * K)) ** 0.5
        W1 = jax.random.uniform(k3, (K, IN_CH, HID_CH), jnp.float32, -s1, s1)
        b1 = jax.random.uniform(k4, (HID_CH,), jnp.float32, -s1, s1)
        W2 = jax.random.uniform(k5, (K, HID_CH, IN_CH), jnp.float32, -s2, s2)
        b2 = jax.random.uniform(k6, (IN_CH,), jnp.float32, -s2, s2)
        return {'x': x, 'edge_index': edge_index, 'W1': W1, 'b1': b1, 'W2': W2, 'b2': b2}
    _L3_gnn_all = _L3_gnn_setup()
    _L3_gnn_in = {k: v for k, v in _L3_gnn_all.items() if k in ('W1', 'b1', 'W2', 'b2')}
    del _L3_gnn_all
    return {'x': x, 'src': src, 'dst': dst, 'edge_attr3_10x16': edge_attr3_10x16, 'edge_weight': edge_weight, 'L0_gnn_W1': _L0_gnn_in['W1'], 'L0_gnn_b1': _L0_gnn_in['b1'], 'L0_gnn_W2': _L0_gnn_in['W2'], 'L0_gnn_b2': _L0_gnn_in['b2'], 'L1_gnn_W_self': _L1_gnn_in['W_self'], 'L1_gnn_b_self': _L1_gnn_in['b_self'], 'L1_gnn_W_neigh': _L1_gnn_in['W_neigh'], 'L1_gnn_b_neigh': _L1_gnn_in['b_neigh'], 'L2_gnn_w_s': _L2_gnn_in['w_s'], 'L2_gnn_w_n': _L2_gnn_in['w_n'], 'L3_gnn_W1': _L3_gnn_in['W1'], 'L3_gnn_b1': _L3_gnn_in['b1'], 'L3_gnn_W2': _L3_gnn_in['W2'], 'L3_gnn_b2': _L3_gnn_in['b2']}

def reference(x, src, dst, edge_attr3_10x16, edge_weight, L0_gnn_W1, L0_gnn_b1, L0_gnn_W2, L0_gnn_b2, L1_gnn_W_self, L1_gnn_b_self, L1_gnn_W_neigh, L1_gnn_b_neigh, L2_gnn_w_s, L2_gnn_w_n, L3_gnn_W1, L3_gnn_b1, L3_gnn_W2, L3_gnn_b2):
    import jax
    import jax.numpy as jnp

    def _L0_gnn_ref(v, e, edge_index, W1, b1, W2, b2):
        import jax, jax.numpy as jnp
        import numpy as np
        LOG2 = 0.6931471805599453
        N_NODES = 50000
        N_EDGES = 500000
        NUM_HEADS = 10
        NUM_FILTERS = 16
        HIDDEN = 128
        i = edge_index[1]
        E = e.shape[0]
        e_flat = e.reshape(E, -1)
        agg = jax.ops.segment_sum(e_flat, i, num_segments=v.shape[0])
        h = agg @ W1.T + b1
        h = jax.nn.softplus(h) - LOG2
        h = h @ W2.T + b2
        return v + h

    def _L1_gnn_ref(feat, edge_weight, src_idx, dst_idx, W_self, b_self, W_neigh, b_neigh):
        import jax, jax.numpy as jnp
        import numpy as np
        N_NODES = 50000
        N_EDGES = 12500
        D_IN = 128
        D_OUT = 128
        msgs = feat[src_idx] * edge_weight[:, None]
        neigh = jax.ops.segment_sum(msgs, dst_idx, num_segments=feat.shape[0])
        ws = jax.ops.segment_sum(edge_weight, dst_idx, num_segments=feat.shape[0])
        h_neigh = neigh / jnp.maximum(ws, 1.0)[:, None]
        rst = (feat @ W_self.T + b_self + h_neigh @ W_neigh.T + b_neigh) / 2.0
        return rst

    def _L2_gnn_ref(features, w_s, w_n, src, dst):
        import jax, jax.numpy as jnp
        import numpy as np
        N_NODES = 100000
        N_EDGES = 25000
        F_IN = 128
        F_OUT = 128
        self_conv = features @ w_s
        nbr_conv = features @ w_n
        messages = nbr_conv[src]
        n = features.shape[0]
        agg = jax.ops.segment_sum(messages, dst, num_segments=n)
        return jax.nn.relu(self_conv + agg)

    def _L3_gnn_ref(x, edge_index, W1, b1, W2, b2):
        import jax, jax.numpy as jnp
        import numpy as np
        N_NODES = 30000
        IN_CH = 128
        HID_CH = 256
        K = 3
        N_EDGES = 7500

        def _norm_weights(edge_index, n):
            src, dst = (edge_index[0], edge_index[1])
            mask = src != dst
            ones = jnp.where(mask, 1.0, 0.0)
            deg = jax.ops.segment_sum(ones, src, num_segments=n)
            dis = jnp.where(deg > 0, deg ** (-0.5), 0.0)
            w = jnp.where(mask, -dis[src] * dis[dst], 0.0)
            return (src, dst, w)

        def _cheb_conv(x, src, dst, w, W, b, n):

            def lap(h):
                return jax.ops.segment_sum(w[:, None] * h[src], dst, num_segments=n)
            Tx_prev = x
            out = x @ W[0]
            if W.shape[0] > 1:
                Tx_cur = lap(x)
                out = out + Tx_cur @ W[1]
                for k in range(2, W.shape[0]):
                    Tx_next = 2.0 * lap(Tx_cur) - Tx_prev
                    out = out + Tx_next @ W[k]
                    Tx_prev, Tx_cur = (Tx_cur, Tx_next)
            return out + b
        n = x.shape[0]
        src, dst, w = _norm_weights(edge_index, n)
        h = jax.nn.relu(_cheb_conv(x, src, dst, w, W1, b1, n))
        return _cheb_conv(h, src, dst, w, W2, b2, n)
    edge_index = jnp.stack([src, dst])
    x = _layernorm(x + _L0_gnn_ref(x, edge_attr3_10x16, edge_index, L0_gnn_W1, L0_gnn_b1, L0_gnn_W2, L0_gnn_b2), axis=-1)
    x = _layernorm(x + _L1_gnn_ref(x, edge_weight, src, dst, L1_gnn_W_self, L1_gnn_b_self, L1_gnn_W_neigh, L1_gnn_b_neigh), axis=-1)
    x = _layernorm(x + _L2_gnn_ref(x, L2_gnn_w_s, L2_gnn_w_n, src, dst), axis=-1)
    x = _layernorm(x + _L3_gnn_ref(x, edge_index, L3_gnn_W1, L3_gnn_b1, L3_gnn_W2, L3_gnn_b2), axis=-1)
    return x

_drawn_inputs = setup_inputs


def setup_inputs(seed=0):
    import zlib

    import numpy as np

    out = dict(_drawn_inputs(seed))
    spreads = {'L0_gnn_b1': (0.0, 0.1),
     'L0_gnn_b2': (0.0, 0.1),
     'L1_gnn_b_self': (0.0, 0.1),
     'L1_gnn_b_neigh': (0.0, 0.1)}
    factors = {'L3_gnn_b1': 6.248}
    for name, (base, spread) in spreads.items():
        noise = np.random.default_rng([zlib.crc32(name.encode()), seed]).standard_normal(out[name].shape)
        drawn = base * np.exp(spread * noise) if base else spread * noise
        out[name] = jnp.asarray(drawn.astype(out[name].dtype))
    for name, factor in factors.items():
        out[name] = (out[name] * factor).astype(out[name].dtype)
    return out
```

```python
from contextlib import ExitStack

import concourse.bass as bass
from concourse import mybir

F32 = mybir.dt.float32
F16 = mybir.dt.float16
I32 = mybir.dt.int32
ALU = mybir.AluOpType
ACT = mybir.ActivationFunctionType

P = 128
NODES = 100000
EDGES = 25000
ATTR = 160
HID = 256
TILES = -(-EDGES // P)
QUADS = TILES // 4
SLOTS = TILES * P
FULL = EDGES // P
REST = EDGES - FULL * P
BLOCKS = -(-NODES // 512)
LAST_BLOCK = NODES - 512
PAD = 1 << 20
BINS = -(-NODES // P)
EPS = 1e-5
assert TILES == 4 * QUADS and QUADS % 2 == 1 and BLOCKS % 2 == 0


class Turn:

    def __init__(self, reg, c):
        self.reg, self.c, self.b = reg, c, c & 1

    def less(self, k):
        return Turn(self.reg, self.c - k)

    def lin(self, scale, add=0):
        if self.reg is None:
            return scale * self.c + add
        r, k = (self.reg if scale == 1 else self.reg * scale), scale * self.c + add
        return r + k if k else r

    def inside(self, n):
        return self.reg is not None or 0 <= self.c < n


class Signal:

    def __init__(self, sem, per, turns):
        self.sem, self.per, self.start, at = sem, per, {}, 0
        for p, n in per.items():
            self.start[p] = at
            at += turns[p] * n

    def value(self, p, g, back=0, k=None):
        return g.less(back).lin(self.per[p], self.start[p] + (self.per[p] if k is None else k))

    def wait(self, eng, p, g, back=0, k=None):
        if g.reg is not None or g.c >= back:
            eng.wait_ge(self.sem, self.value(p, g, back, k))


class Transfer:

    def __init__(self, sems, n, turns):
        self.sems, self.n, self.start, self.end, at = sems, n, {}, {}, [0, 0]
        for p in n:
            self.start[p] = tuple(at)
            at = [at[b] + 16 * n[p] * ((turns[p] + 1 - b) // 2) for b in range(2)]
            self.end[p] = tuple(at)

    def wait(self, eng, p, g, back=0):
        if g.reg is not None or g.c >= back:
            g, n = g.less(back), self.n[p]
            eng.wait_ge(self.sems[g.b], g.lin(8 * n, self.start[p][g.b] + 16 * n - 8 * n * g.b))

    def wait_all(self, eng, p):
        for b in range(2):
            eng.wait_ge(self.sems[b], self.end[p][b])


class Count:

    def __init__(self, eng, name, what, behind=0):
        self.eng, self.reg, self.what, self.behind = eng, eng.alloc_register(name), what, behind

    def begin(self, p, g):
        self.eng.reg_mov(self.reg, self.what.value(p, g, self.behind))

    def wait(self, p, g):
        if g.reg is None:
            self.what.wait(self.eng, p, g)
        else:
            self.eng.wait_ge(self.what.sem, self.reg)
            self.eng.reg_add(self.reg, self.reg, self.what.per[p])


def run_turns(eng, p, n, lead, tail, body, counts=(), last=1):
    end = (n - last) // 2 * 2
    for c in range(lead):
        body(Turn(None, c))
    for count in counts:
        count.begin(p, Turn(None, lead))
    with eng.Fori(lead, end - 1, 2) as i:
        body(Turn(i, 0))
        body(Turn(i, 1))
    for c in range(end, n + tail):
        body(Turn(None, c))


def gnn_kernel(nc, x, src, dst, attr, ew, W1, b1, W2, b2, Wself, bself, Wneigh, bneigh, ws, wn, G1, gb1, G2, gb2, out):
    ctx = ExitStack()
    with ctx:
        def sb(name, shape, dt=F32):
            return ctx.enter_context(nc.sbuf_tensor(name, shape, dt))

        def sem(name):
            return ctx.enter_context(nc.semaphore(name))

        def dram(name, shape):
            return nc.dram_tensor(name, shape, F32).ap()

        state1, state2, state3 = (dram(f"state{n}", (2 * SLOTS, P)) for n in (1, 2, 3))
        state_h = dram("state_h", (2 * SLOTS, HID))
        lap1, lap2 = dram("lap1", (SLOTS + P, P)), dram("lap2", (SLOTS + P, P))
        lap1_cols = dram("lap1_cols", (QUADS, P, 512))
        near_out, most_out = dram("near_out", (SLOTS, P)), dram("most_out", (SLOTS, P))
        node_table = dram("node_table", (P * BINS, 2))

        def one(v, g):
            return v[g.c] if g.reg is None else v[bass.ds(g.lin(1), 1)].rearrange("a p k d -> (a p) k d")

        def quad_of(t, g, half=0):
            return one(t[half * SLOTS:(half + 1) * SLOTS, :].rearrange("(q p k) d -> q p k d", p=P, k=4), g)

        def block_of(t, g):
            if g.reg is None and g.c == BLOCKS - 1:
                return t[LAST_BLOCK:NODES, :].rearrange("(p k) d -> p k d", k=4)
            return one(t[0:(BLOCKS - 1) * 512, :].rearrange("(q p k) d -> q p k d", p=P, k=4), g)

        dst_row = sb("dst_row", [P, 1 + SLOTS], I32)
        dst_col, ew_col, lap_w, mask = (sb(n, [P, TILES]) for n in ("dst_col", "ew_col", "lap_w", "mask"))
        src_g, dst_g, rows_of_src, rows_of_lap, out_row = (
            sb(n, [P, TILES], I32) for n in ("src_g", "dst_g", "rows_of_src", "rows_of_lap", "out_row"))
        look_idx = sb("look_idx", [P, TILES, 2], I32)
        looked = sb("looked", [P, TILES, 4])
        zero_i = sb("zero_i", [P, 4], I32)
        ident, center, half_center, ones, A1, wn_c, ws_sb, wn_sb, W1Ta, W2T = (
            sb(n, [P, P]) for n in ("ident", "center", "half_center", "ones", "A1", "wn_c", "ws_sb", "wn_sb", "W1Ta", "W2T"))
        W1Tb = sb("W1Tb", [32, P])
        G02, Gm1, G2x2 = (sb(n, [P, HID]) for n in ("G02", "Gm1", "G2x2"))
        V02 = sb("V02", [P, 2, P])
        V12 = sb("V12", [P, 2, HID])
        c0h, b1c, b2h, gb2_row = (sb(n, [P, P]) for n in ("c0h", "b1c", "b2h", "gb2_row"))
        gb1_row = sb("gb1_row", [P, HID])
        gb1_col = sb("gb1_col", [P, 2])
        b1_col, bs_col, bn_col, sp_col = (sb(n, [P, 1]) for n in ("b1_col", "bs_col", "bn_col", "sp_col"))
        consts = sb("consts", [P, 4])
        EPS4, EPS1, EPS2, HALF = (consts[:, n:n + 1] for n in range(4))

        xin, y0, y1, u2, x3, x3b, outb = (sb(n, [P, 2, 4, P]) for n in ("xin", "y0", "y1", "u2", "x3", "x3b", "outb"))
        yTa, yTb, yTc, y3 = (sb(n, [P, 4, P]) for n in ("yTa", "yTb", "yTc", "y3"))
        hT = sb("hT", [P, 2, 4, P])
        rows, hb = (sb(n, [P, 2, 4, HID]) for n in ("rows", "hb"))
        cont = sb("cont", [P, 2, 4, P], F16)
        zeros = sb("zeros", [P, P])
        unused = sb("unused", [P, 4, P], mybir.dt.bfloat16)
        ssum, tmpv, negm = (sb(n, [P, 2, 4]) for n in ("ssum", "tmpv", "negm"))
        bn = sb("bn", [P, 3, 4, 6])
        mv = sb("mv", [P, 3, 2, 4, 2])
        sd, rs = sb("sd", [P, 4, 2, 4]), sb("rs", [P, 4, 2, 4])
        idx, idx_out = sb("idx", [P, 2, 4], I32), sb("idx_out", [P, 2, 4], I32)
        lk = sb("lk", [P, 2, 4])
        sel, agg_a, agg_b, lap_in = u2, x3, x3b, y0

        ps = ctx.enter_context(nc.psum_tensor("ps", [P, 8, 512], F32))

        def bank(n):
            return ps[:, n, :].rearrange("p (k d) -> p k d", k=4)

        def wide(n):
            return ps[:, n:n + 2, :].rearrange("p n (k d) -> p (n k) d", d=HID)

        def all4(row):
            return row.unsqueeze(1).to_broadcast([P, 4, row.shape[1]])

        turns = {"tgt0": QUADS, "src0": QUADS, "nodes": BLOCKS, "index": 0, "L1": QUADS, "L2": QUADS, "T1": QUADS,
                 "T2": QUADS, "LH": QUADS, "LU": QUADS}
        PASSES = list(turns)
        AGG = ["tgt0", "L1", "L2", "T1", "T2", "LH", "LU"]

        def signal(name, per):
            per = per if isinstance(per, dict) else {p: 1 for p in per.split()}
            return Signal(sem(name), per, turns)

        def transfer(name, **n):
            return Transfer([sem(name + "_even"), sem(name + "_odd")], n, turns)

        x_gathered = transfer("x_gathered", tgt0=4, src0=4)
        attr_in = transfer("attr_in", tgt0=1)
        out_scattered = transfer("out_scattered", LU=4)
        x_in = transfer("x_in", nodes=1, L1=1, L2=1, T2=1, LH=1, LU=1)
        rows_in = transfer("rows_in", L1=4, L2=4, T1=4, T2=4, LH=4, LU=4)
        tail_in = sem("tail_in")
        look_in = transfer("look_in", nodes=2)
        lap_arrived = transfer("lap_arrived", T2=1)
        out_st = transfer("out_st", tgt0=1, src0=1, nodes=1, L1=1, L2=1, T1=1, T2=1, LH=1)
        more_st = transfer("more_st", src0=1, T1=1, T2=1, LH=1)
        x3_st = transfer("x3_st", src0=1)
        h_st = transfer("h_st", src0=1)
        staged = signal("staged", "tgt0 src0 nodes L1 L2 T1 T2 LH LU")
        out_staged = signal("out_staged", "LU")
        y0_made = signal("y0_made", "src0 nodes")
        x3_made = signal("x3_made", "src0 nodes")
        x3b_made = signal("x3b_made", "nodes")
        bn0, mv0, rs0, y1_made = (signal(n, "src0 nodes") for n in ("bn0", "mv0", "rs0", "y1_made"))
        u2_made, bn2, mv2, tv2, rs2 = (signal(n, "src0 nodes") for n in ("u2_made", "bn2", "mv2", "tv2", "rs2"))
        y3_made, bn3, mv3, rs3, looked_up = (signal(n, "nodes") for n in ("y3_made", "bn3", "mv3", "rs3", "looked_up"))
        x1_made, rs1, x2_made, h_biased = (signal(n, "src0") for n in ("x1_made", "rs1", "x2_made", "h_biased"))
        selected = signal("selected", {p: 1 for p in AGG})
        carried = signal("carried", {p: 8 if p in ("tgt0", "L1", "LH") else 4 for p in AGG})
        step = signal("step", {"tgt0": 2, "L1": 4, "L2": 1, "T2": 1, "LU": 1})
        softplus_in, softplus_made = signal("softplus_in", "tgt0"), signal("softplus_made", "tgt0")
        bn_e, mv_e = signal("bn_e", "tgt0 L1 L2 LU"), signal("mv_e", "tgt0 L1 L2 LU")
        rs_e = signal("rs_e", "L1 L2 LU")
        out_made = signal("out_made", "tgt0 nodes L1 L2 T2 LH LU")
        y0T_kept, sd0, y1T_kept, squared, x3T_kept, sd2 = (
            signal(n, "src0 nodes") for n in ("y0T_kept", "sd0", "y1T_kept", "squared", "x3T_kept", "sd2"))
        sd1, h_kept = signal("sd1", "src0"), signal("h_kept", "src0 T2")
        sd3 = signal("sd3", "nodes")
        hidden = signal("hidden", {"nodes": 2, "T2": 2})
        softplus = signal("softplus", {"tgt0": 4})
        sd_e = signal("sd_e", "tgt0 L1 L2 LU")
        turned_kept = signal("turned_kept", "L1 L2 T1 T2")
        u_kept = signal("u_kept", "LH")
        y0_turned, p1_made, y1_turned, p2_made, x3_turned, h_made = (
            signal(n, "src0 nodes") for n in ("y0_turned", "p1_made", "y1_turned", "p2_made", "x3_turned", "h_made"))
        p3_made = signal("p3_made", "nodes")
        summed = signal("summed", {p: 1 for p in AGG})
        turned = signal("turned", "L1 L2 T1 T2 LU")
        first_product = signal("first_product", "tgt0 T2")
        product = signal("product", "tgt0 L1 L2 T2 LH")
        h_turned = signal("h_turned", "T2")
        loaded, pads, zeroed, tables_st, fixed, vstep, tstep, astep, pstep, alink, dlink, roots_in, hots, counted = (
            sem(n) for n in ("loaded", "pads", "zeroed", "tables_st", "fixed", "vstep", "tstep", "astep", "pstep",
                             "alink", "dlink", "roots_in", "hots", "counted"))
        seam = sem("seam")

        def enter(eng, p):
            eng.wait_ge(seam, 5 * (PASSES.index(p) + 1))

        def skip(eng, p):
            enter(eng, p)
            leave(eng)

        def leave(eng):
            eng.drain().then_inc(seam, 1)

        def flat(t):
            return t[:].rearrange("p a k d -> p (a k d)")

        def cols(t, n, dt=F32):
            v = flat(t)[:, n * TILES:(n + 1) * TILES]
            return v if dt == F32 else v.bitcast(dt)

        src_i, dst_i, nxt_i, t_i, s_i = (cols(xin, n, I32) for n in range(5))
        a_src, b_src, a_dst, b_dst, rep = (cols(y0, n) for n in range(5))
        v_tile, v_lane, src_f, nxt_f = (cols(y1, n) for n in range(4))
        s2_i, t_f, has = cols(outb, 0, I32), cols(outb, 1), cols(outb, 2)
        hot = hb[:].rearrange("p a k d -> p (a k d)").bitcast(F16)
        hot_bin = [[hot[:, (2 * b + j) * BINS:(2 * b + j + 1) * BINS] for j in range(2)] for b in range(2)]
        hot_lane = [[hot[:, 4 * BINS + (3 * b + j) * P:4 * BINS + (3 * b + j + 1) * P] for j in range(3)] for b in range(2)]
        iotas = y3[:].rearrange("p k d -> p (k d)").bitcast(F16)
        iota_bin, iota_lane = iotas[:, 0:BINS], iotas[:, BINS:BINS + P]
        table = rows[:].rearrange("p a k d -> p (a k d)")[:, 0:2 * BINS].rearrange("p (n c) -> p n c", c=2)
        raw_G1 = flat(x3)[:, 0:3 * HID].rearrange("p (n d) -> p n d", n=3)
        raw_G2 = flat(x3b)[:, 0:6 * P].rearrange("p (n d) -> p n d", n=6)
        raw = yTa[:].rearrange("p k d -> p (k d)")
        raw_W1, raw_W2, raw_Ws = raw[:, 0:ATTR], raw[:, ATTR:ATTR + P], raw[:, ATTR + P:ATTR + 2 * P]
        raw_Wn, Bm, BtC, bcol = (yTb[:, n, :] for n in range(4))
        spb, = (yTc[:, n, :] for n in range(1))
        LOADS = 24
        V_COLS, V_WEIGHTS, V_BTC, V_TABLE = 1, 2, 3, 4

        block = ctx.enter_context(nc.Block())

        @block.sync
        def _(sp):
            def load(dst_ap, src_ap):
                sp.dma_start(dst_ap, src_ap).then_inc(loaded, 16)

            def row(v):
                return v.rearrange("(a n) -> a n", a=1)

            with nc.allow_non_contiguous_dma("edge lists with an edge per partition; columns of biases"):
                sp.wait_ge(pads, 1)
                for t, s, n in ((src_i, src, EDGES), (dst_i, dst, EDGES), (nxt_i, dst[1:EDGES], EDGES - 1),
                                (ew_col, ew, EDGES)):
                    load(t[:, 0:FULL], s[0:FULL * P].rearrange("(t p) -> p t", p=P))
                    load(t[0:n - FULL * P, FULL:TILES], s[FULL * P:n].rearrange("(p t) -> p t", t=1))
                load(dst_row[:, 1:1 + EDGES], row(dst).to_broadcast([P, EDGES]))
                load(raw_W1, W1)
                load(raw_W2, W2)
                load(raw_Ws, Wself)
                load(raw_Wn, Wneigh)
                load(ws_sb[:, :], ws)
                load(wn_sb[:, :], wn)
                load(raw_G1, G1.rearrange("n p d -> p n d"))
                load(raw_G2, G2.rearrange("n (j p) d -> p (n j) d", p=P))
                for t, s in ((b1_col, b1), (bs_col, bself), (bn_col, bneigh)):
                    load(t[:, :], s.rearrange("(p a) -> p a", a=1))
                load(gb1_col[:, :], gb1.rearrange("(j p) -> p j", p=P))
                load(b2h[:, :], row(b2).to_broadcast([P, P]))
                load(gb2_row[:, :], row(gb2).to_broadcast([P, P]))
                load(gb1_row[:, :], row(gb1).to_broadcast([P, HID]))
            sp.wait_ge(fixed, 1)
            sp.dma_start(lap1[SLOTS:SLOTS + P, :], zeros[:, :]).then_inc(tables_st, 16)
            sp.dma_start(lap2[SLOTS:SLOTS + P, :], zeros[:, :]).then_inc(tables_st, 16)
            sp.wait_ge(vstep, V_TABLE)
            sp.dma_start(node_table.rearrange("(p n) c -> p n c", p=P), table).then_inc(tables_st, 16)
            sp.wait_ge(loaded, 16 * LOADS)
            sp.wait_ge(tables_st, 48)
            leave(sp)

            def edge_pass(p, state=None, half=0, store=None):
                def state_load(g):
                    if state is not None and g.inside(QUADS):
                        if p == "L1":
                            turned.wait(sp, p, g, back=2)
                        if p in ("L2", "LU"):
                            step.wait(sp, p, g, back=2, k=1)
                        if p in ("T2", "LH"):
                            out_made.wait(sp, p, g, back=2)
                        sp.dma_start(xin[:, g.b], quad_of(state, g, half)).then_inc(x_in.sems[g.b], 16)
                        if p == "T2":
                            first_product.wait(sp, p, g, back=2)
                            v = lap1_cols.rearrange("q p (k d) -> q p k d", k=4)
                            sp.dma_start(lap_in[:, g.b], one(v, g)).then_inc(lap_arrived.sems[g.b], 16)

                def turn(g):
                    state_load(g.less(-1))
                    if p == "T1":
                        carried.wait(sp, p, g)
                        v = lap1_cols.rearrange("q p (k d) -> q p k d", k=4)
                        sp.dma_start(one(v, g), agg_a[:, g.b]).then_inc(more_st.sems[g.b], 16)
                        turned_kept.wait(sp, p, g)
                    elif p != "LU":
                        out_made.wait(sp, p, g)
                    if store is not None:
                        sp.dma_start(quad_of(store, g), outb[:, g.b]).then_inc(out_st.sems[g.b], 16)
                    if p == "T2":
                        h_kept.wait(sp, p, g)
                        sp.dma_start(quad_of(state_h, g), hb[:, g.b]).then_inc(more_st.sems[g.b], 16)
                    if p == "LH":
                        u_kept.wait(sp, p, g)
                        sp.dma_start(quad_of(lap2, g), y1[:, g.b]).then_inc(more_st.sems[g.b], 16)

                enter(sp, p)
                state_load(Turn(None, 0))
                run_turns(sp, p, QUADS, 2, 0, turn)
                if store is not None:
                    out_st.wait_all(sp, p)
                if p in more_st.n:
                    more_st.wait_all(sp, p)
                leave(sp)

            def attr_load(g):
                if not g.inside(QUADS):
                    return
                summed.wait(sp, "tgt0", g, back=2)
                if g.reg is None and g.c == QUADS - 1:
                    v = attr[(QUADS - 1) * 512:FULL * P, :].rearrange("(k p) d -> p k d", p=P)
                    sp.dma_start(rows[:, g.b, 0:3, 0:ATTR], v).then_inc(attr_in.sems[g.b], 16)
                    sp.wait_ge(zeroed, 1)
                    sp.dma_start(rows[0:REST, g.b, 3, 0:ATTR], attr[FULL * P:EDGES, :]).then_inc(tail_in, 16)
                else:
                    v = attr[0:(QUADS - 1) * 512, :].rearrange("(q k p) d -> q p k d", p=P, k=4)
                    sp.dma_start(rows[:, g.b, :, 0:ATTR], one(v, g)).then_inc(attr_in.sems[g.b], 16)

            def tgt0_turn(g):
                attr_load(g.less(-1))
                out_made.wait(sp, "tgt0", g)
                sp.dma_start(quad_of(state1, g), outb[:, g.b]).then_inc(out_st.sems[g.b], 16)

            enter(sp, "tgt0")
            attr_load(Turn(None, 0))
            run_turns(sp, "tgt0", QUADS, 2, 0, tgt0_turn, last=3)
            out_st.wait_all(sp, "tgt0")
            leave(sp)

            def src0_turn(g):
                for signal_, g_, t, buf, tr in ((x1_made, g, state1, outb, out_st), (x2_made, g.less(1), state2, x3b, more_st),
                                                (x3_made, g.less(2), state3, x3, x3_st), (h_kept, g.less(3), state_h, hb, h_st)):
                    if g_.inside(QUADS):
                        signal_.wait(sp, "src0", g_)
                        sp.dma_start(quad_of(t, g_, 1), buf[:, g_.b]).then_inc(tr.sems[g_.b], 16)

            enter(sp, "src0")
            run_turns(sp, "src0", QUADS, 6, 4, src0_turn)
            for tr in (out_st, more_st, x3_st, h_st):
                tr.wait_all(sp, "src0")
            leave(sp)

            def x_load(g):
                if g.inside(BLOCKS):
                    y0_made.wait(sp, "nodes", g, back=2)
                    sp.dma_start(xin[:, g.b], block_of(x, g)).then_inc(x_in.sems[g.b], 16)

            def nodes_turn(g):
                x_load(g.less(-1))
                g4 = g.less(4)
                if g4.inside(BLOCKS):
                    out_made.wait(sp, "nodes", g4)
                    if g4.reg is None and g4.c == BLOCKS - 1:
                        out_st.wait(sp, "nodes", g4, back=1)
                    sp.dma_start(block_of(out, g4), outb[:, g4.b]).then_inc(out_st.sems[g4.b], 16)

            enter(sp, "nodes")
            x_load(Turn(None, 0))
            run_turns(sp, "nodes", BLOCKS, 6, 4, nodes_turn)
            out_st.wait_all(sp, "nodes")
            leave(sp)
            skip(sp, "index")

            edge_pass("L1", state1, store=state2)
            edge_pass("L2", state2, store=state3)
            edge_pass("T1", store=lap1)
            edge_pass("T2", state3, store=near_out)
            edge_pass("LH", near_out, store=most_out)
            edge_pass("LU", most_out)

        @block.gpsimd
        def _(pool):
            gp = nc.gpsimd
            gp.memset(zeros[:, :], 0.0).then_inc(pstep, 1)
            gp.memset(ident[:, :], 0.0)
            gp.memset(zero_i[:, :], 0)
            gp.memset(ones[:, :], 1.0).then_inc(pstep, 1)
            for n, v in enumerate((EPS / 4, EPS, EPS * EPS, 0.5)):
                gp.memset(consts[:, n:n + 1], v)
            pool.wait_ge(pstep, 2)
            gp.affine_select(out=ident[:, :], in_=ident[:, :], compare_op=ALU.not_equal, fill=1.0, base=0,
                             pattern=[[-1, P]], channel_multiplier=1).then_inc(pstep, 1)
            gp.iota(rows_of_src[:, :], pattern=[[512, QUADS], [1, 4]], base=SLOTS, channel_multiplier=4)
            gp.iota(rows_of_lap[:, :], pattern=[[0, TILES]], base=SLOTS, channel_multiplier=1)
            gp.iota(s2_i, pattern=[[1, TILES]], base=1, channel_multiplier=0)
            gp.iota(s_i, pattern=[[0, TILES]], base=0, channel_multiplier=1)
            gp.iota(flat(u2)[:, 0:BINS].bitcast(I32), pattern=[[1, BINS]], base=0, channel_multiplier=0).then_inc(pstep, 1)
            pool.wait_ge(pstep, 4)
            gp.drain().then_inc(fixed, 1)
            leave(pool)

            staged_count = Count(pool, "staged_count", staged)
            rs2_count = Count(pool, "rs2_count", rs2, behind=2)
            out_count = Count(pool, "out_count", out_made)

            def gather(p, g, table_, index, dest, width, sems, waits):
                for s, back in waits:
                    s.wait(pool, p, g, back=back)
                gp.tensor_tensor(idx[:, g.b, :], index[:, bass.ds(g.lin(4), 4)], zero_i[:, :], ALU.add)\
                    .then_inc(staged.sem, 1)
                staged_count.wait(p, g)
                for k in range(4):
                    gp.indirect_dma_start(out=dest[:, g.b, k, 0:width], out_offset=None, in_=table_,
                                          in_offset=bass.IndirectOffsetOnAxis(ap=idx[:, g.b, k:k + 1], axis=0))\
                        .then_inc(sems.sems[g.b], 16)

            enter(pool, "tgt0")
            def tgt0_turn(g):
                gather("tgt0", g, x, dst_g, xin, P, x_gathered, [(step, 2)])
                if g.reg is None and g.c == QUADS - 1:
                    summed.wait(pool, "tgt0", g, back=2)
                    gp.memset(rows[:, g.b, 3, 0:ATTR], 0.0).then_inc(zeroed, 1)

            run_turns(pool, "tgt0", QUADS, 2, 0, tgt0_turn, [staged_count])
            leave(pool)

            def row_pass(p, n, before):
                def turn(g):
                    before(g)
                    g2, g3 = g.less(2), g.less(3)
                    if g.inside(n):
                        (x_in if p == "nodes" else x_gathered).wait(pool, p, g)
                        y0_turned.wait(pool, p, g, back=2)
                        bn0.wait(pool, p, g, back=2)
                        if p == "src0":
                            x1_made.wait(pool, p, g, back=2)
                        gp.tensor_tensor(y0[:, g.b], xin[:, g.b], all4(c0h[:, :]), ALU.add).then_inc(y0_made.sem, 1)
                    if g2.inside(n):
                        x3_turned.wait(pool, p, g2, back=2)
                        (x3_st if p == "src0" else x3b_made).wait(pool, p, g2, back=2)
                        rs2_count.wait(p, g2)
                        for k in range(4):
                            i = gp.tensor_scalar(x3[:, g2.b, k, :], u2[:, g2.b, k, :], negm[:, g2.b, k:k + 1],
                                                 rs[:, 2, g2.b, k:k + 1], ALU.add, ALU.mult)
                        i.then_inc(x3_made.sem, 1)
                    if p == "nodes" and g3.inside(n):
                        x3_made.wait(pool, p, g3)
                        y3_made.wait(pool, p, g3, back=2)
                        gp.tensor_tensor(x3b[:, g3.b], x3[:, g3.b], all4(gb2_row[:, :]), ALU.add).then_inc(x3b_made.sem, 1)
                return turn

            def src_rows(g):
                g = g.less(-1)
                if g.inside(QUADS):
                    gather("src0", g, x, src_g, xin, P, x_gathered, [(y0_made, 2)])

            enter(pool, "src0")
            gather("src0", Turn(None, 0), x, src_g, xin, P, x_gathered, [])
            staged_count.behind = -1
            run_turns(pool, "src0", QUADS, 6, 4, row_pass("src0", QUADS, src_rows), [staged_count, rs2_count])
            staged_count.behind = 0
            leave(pool)

            def look(g):
                if g.inside(BLOCKS):
                    look_in.wait(pool, "nodes", g, back=2)
                    looked_up.wait(pool, "nodes", g, back=2)
                    gp.tensor_tensor(idx[:, g.b, 0:2], look_idx[:, bass.ds(g.lin(1), 1), :].rearrange("p a c -> p (a c)"),
                                     zero_i[:, 0:2], ALU.add).then_inc(staged.sem, 1)
                    staged_count.wait("nodes", g)
                    for j in range(2):
                        gp.indirect_dma_start(out=lk[:, g.b, 2 * j:2 * j + 2], out_offset=None, in_=node_table,
                                              in_offset=bass.IndirectOffsetOnAxis(ap=idx[:, g.b, j:j + 1], axis=0))\
                            .then_inc(look_in.sems[g.b], 16)

            assert BLOCKS == TILES
            enter(pool, "nodes")
            run_turns(pool, "nodes", BLOCKS, 6, 4, row_pass("nodes", BLOCKS, look), [staged_count, rs2_count])
            leave(pool)
            skip(pool, "index")

            def edge_pass(p, table_, index, width=P):
                enter(pool, p)
                run_turns(pool, p, QUADS, 2, 0,
                          lambda g: gather(p, g, table_, index, rows, width, rows_in, [(summed, 2)]), [staged_count])
                leave(pool)

            edge_pass("L1", state1, rows_of_src)
            edge_pass("L2", state2, rows_of_src)
            edge_pass("T1", state3, rows_of_src)
            edge_pass("T2", lap1, rows_of_lap)
            edge_pass("LH", state_h, rows_of_src, HID)

            def last_turn(g):
                if g.less(-1).inside(QUADS):
                    gather("LU", g.less(-1), lap2, rows_of_lap, rows, P, rows_in, [(summed, 2)])
                out_scattered.wait(pool, "LU", g, back=2)
                gp.tensor_tensor(idx_out[:, g.b, :], out_row[:, bass.ds(g.lin(4), 4)], zero_i[:, :], ALU.add)\
                    .then_inc(out_staged.sem, 1)
                out_staged.wait(pool, "LU", g)
                out_count.wait("LU", g)
                for k in range(4):
                    gp.indirect_dma_start(out=out, in_=outb[:, g.b, k, :], in_offset=None, bounds_check=NODES - 1,
                                          oob_is_err=False,
                                          out_offset=bass.IndirectOffsetOnAxis(ap=idx_out[:, g.b, k:k + 1], axis=0))\
                        .then_inc(out_scattered.sems[g.b], 16)

            enter(pool, "LU")
            gather("LU", Turn(None, 0), lap2, rows_of_lap, rows, P, rows_in, [])
            staged_count.behind = -1
            run_turns(pool, "LU", QUADS, 2, 0, last_turn, [staged_count, out_count])
            out_scattered.wait_all(pool, "LU")

        @block.vector
        def _(dve):
            v = nc.vector
            links = [0]

            def link(i):
                links[0] += 1
                i.then_inc(dlink, 1)
                dve.wait_ge(dlink, links[0])

            for t in (src_i, dst_i, nxt_i):
                v.memset(t, PAD)
            v.memset(ew_col[:, :], 0.0)
            v.memset(dst_row[:, 0:1], -1)
            v.memset(dst_row[:, 1 + EDGES:], PAD).then_inc(pads, 1)
            dve.wait_ge(fixed, 1)
            dve.wait_ge(loaded, 16 * LOADS)

            v.tensor_copy(src_f, src_i)
            v.tensor_copy(dst_col[:, :], dst_i)
            v.tensor_copy(nxt_f, nxt_i)
            v.tensor_copy(v_tile, s2_i)
            v.tensor_copy(v_lane, s_i)
            v.tensor_copy(iota_bin, flat(u2)[:, 0:BINS].bitcast(I32))
            link(v.tensor_copy(iota_lane, flat(u2)[:, 0:P].bitcast(I32)))
            v.tensor_tensor(mask[:, :], src_f, dst_col[:, :], ALU.not_equal)
            link(v.tensor_tensor(rep, dst_col[:, :], nxt_f, ALU.not_equal))
            v.tensor_tensor(v_tile, v_tile, rep, ALU.mult)
            v.tensor_tensor(v_lane, v_lane, rep, ALU.mult)
            link(v.tensor_scalar(t_f, rep, -float(PAD), float(PAD), ALU.mult, ALU.add))
            v.tensor_tensor(out_row[:, :], t_f, dst_col[:, :], ALU.add)
            for ids, a, b in ((src_i, a_src, b_src), (dst_i, a_dst, b_dst)):
                v.tensor_scalar(t_i, ids, 7, None, ALU.logical_shift_right)
                link(v.tensor_scalar(s_i, ids, P - 1, None, ALU.bitwise_and))
                v.tensor_copy(a, t_i)
                link(v.tensor_copy(b, s_i))
            v.tensor_scalar(src_g[:, :], src_f, float(NODES - 1), None, ALU.min)
            link(v.tensor_scalar(dst_g[:, :], dst_col[:, :], float(NODES - 1), None, ALU.min))
            for j, ids in enumerate((src_g, dst_g)):
                v.tensor_scalar(t_i, ids[:, :], 7, None, ALU.logical_shift_right)
                link(v.tensor_scalar(s_i, ids[:, :], P - 1, None, ALU.bitwise_and))
                link(v.scalar_tensor_tensor(look_idx[:, :, j], s_i, float(BINS), t_i, ALU.mult, ALU.add))

            v.drain().then_inc(vstep, 1)

            def one_hot(g):
                if g.reg is not None or g.c >= 2:
                    dve.wait_ge(counted, g.lin(1, -1))
                c = bass.ds(g.lin(1), 1)
                (bin_s, bin_d), (lane_s, lane_t, lane_l) = hot_bin[g.b], hot_lane[g.b]
                v.tensor_scalar(bin_s, iota_bin, a_src[:, c], None, ALU.is_equal)
                v.tensor_scalar(bin_d, iota_bin, a_dst[:, c], None, ALU.is_equal)
                v.tensor_scalar(lane_s, iota_lane, b_src[:, c], mask[:, c], ALU.is_equal, ALU.mult)
                v.tensor_scalar(lane_t, iota_lane, b_dst[:, c], v_tile[:, c], ALU.is_equal, ALU.mult)
                v.tensor_scalar(lane_l, iota_lane, b_dst[:, c], v_lane[:, c], ALU.is_equal, ALU.mult)\
                    .then_inc(hots, 1)

            run_turns(dve, "", TILES, 2, 0, one_hot)

            v.tensor_scalar(center[:, :], ident[:, :], 1.0, -1.0 / P, ALU.mult, ALU.add)
            v.tensor_scalar(half_center[:, :], ident[:, :], 0.5, -0.5 / P, ALU.mult, ALU.add)
            v.tensor_tensor(G02[:, :], raw_G1[:, 0, :], raw_G1[:, 2, :], ALU.subtract)
            v.tensor_copy(Gm1[:, :], raw_G1[:, 1, :])
            v.tensor_scalar(G2x2[:, :], raw_G1[:, 2, :], 2.0, None, ALU.mult)
            v.tensor_tensor(V02[:, :, :], raw_G2[:, 0:2, :], raw_G2[:, 4:6, :], ALU.subtract)
            v.tensor_copy(V12[:, :, 0:P], raw_G2[:, 2:4, :])
            v.tensor_scalar(V12[:, :, P:HID], raw_G2[:, 4:6, :], 2.0, None, ALU.mult)
            link(v.tensor_tensor(bs_col[:, :], bs_col[:, :], bn_col[:, :], ALU.add))
            v.tensor_scalar(bcol, ones[:, :], bs_col[:, :], None, ALU.mult)
            v.tensor_scalar(b2h[:, :], b2h[:, :], 0.5, None, ALU.mult)
            dve.wait_ge(astep, 1)
            link(v.scalar_tensor_tensor(sp_col[:, :], b1_col[:, :], 0.0, sp_col[:, :], ALU.max, ALU.add))
            v.tensor_scalar(spb, ones[:, :], sp_col[:, :], None, ALU.mult)
            dve.wait_ge(tstep, 2)
            v.tensor_copy(W1Ta[:, :], bank(6)[:, 0, :])
            v.tensor_copy(W1Tb[:, :], ps[0:32, 6, P:2 * P])
            v.tensor_copy(W2T[:, :], bank(6)[:, 2, :])
            v.scalar_tensor_tensor(Bm, bank(6)[:, 3, :], 0.5, ident[:, :], ALU.mult, ALU.add).then_inc(vstep, 1)
            dve.wait_ge(tstep, 3)
            v.tensor_copy(BtC, bank(7)[:, 0, :]).then_inc(vstep, 1)
            v.tensor_copy(wn_c[:, :], bank(7)[:, 1, :])
            v.tensor_copy(b1c[:, :], bank(7)[:, 2, :])
            link(v.scalar_tensor_tensor(c0h[:, :], bank(7)[:, 3, :], 0.5, b2h[:, :], ALU.mult, ALU.add))
            dve.wait_ge(tstep, 4)
            v.tensor_copy(A1[:, :], bank(6)[:, 0, :])
            for lo, n, bk in ((0, 512, 0), (512, BINS - 512, 1)):
                v.tensor_copy(table[:, lo:lo + n, 1], ps[:, 4 + bk, 0:n])
                v.tensor_scalar(flat(x3)[:, lo:lo + n], ps[:, bk, 0:n], 1.0, None, ALU.max)
                link(v.tensor_scalar(flat(x3b)[:, lo:lo + n], ps[:, bk, 0:n], 1.0, None, ALU.min))
                link(v.scalar_tensor_tensor(table[:, lo:lo + n, 0], ps[:, 2 + bk, 0:n], float(P), table[:, lo:lo + n, 1],
                                            ALU.mult, ALU.add))
            v.drain().then_inc(roots_in, 1)
            dve.wait_ge(astep, 2)
            link(v.reciprocal(flat(x3)[:, 0:BINS], flat(x3)[:, 0:BINS]))
            link(v.tensor_tensor(table[:, :, 1], flat(x3)[:, 0:BINS], flat(x3b)[:, 0:BINS], ALU.mult))
            v.drain().then_inc(vstep, 1)
            leave(dve)

            def dev(n, b, k):
                return rs[:, n, b, k:k + 1]

            def edge_pass(p, weight=None):
                bn_count = bn_e_count
                two = carried.per[p] == 8

                def select(g):
                    if not g.inside(QUADS):
                        return
                    summed.wait(dve, p, g, back=2)
                    for k in range(4):
                        r = dst_row[:, bass.ds(g.lin(512, 1 + P * k), P)]
                        v.tensor_scalar(cont[:, g.b, k, :], r, dst_row[:, bass.ds(g.lin(512, P * k), 1)], None, ALU.is_equal)
                        c = bass.ds(g.lin(4, k), 1)
                        if weight is None:
                            i = v.tensor_scalar(sel[:, g.b, k, :], r, dst_col[:, c], None, ALU.is_equal)
                        else:
                            i = v.tensor_scalar(sel[:, g.b, k, :], r, dst_col[:, c], weight[:, c], ALU.is_equal, ALU.mult)
                    i.then_inc(selected.sem, 1)

                def carry(g):
                    summed.wait(dve, p, g)
                    if p in ("L1", "L2", "LH"):
                        product.wait(dve, p, g, back=2)
                    elif p in ("T1", "LU"):
                        turned.wait(dve, p, g, back=2)
                    else:
                        first_product.wait(dve, p, g, back=2)
                    if p == "T1":
                        more_st.wait(dve, p, g, back=2)
                    n = 0
                    parts = [(agg_a, 0, P)] + ([(agg_b, 2, 32 if p == "tgt0" else P)] if two else [])
                    for k in range(4):
                        for t, bk, np_ in parts:
                            if n >= len(parts):
                                carried.wait(dve, p, g, k=n - len(parts) + 1)
                            elif g.reg is not None or g.c > 0:
                                carried.wait(dve, p, g, back=1, k=carried.per[p] - len(parts) + n + 1)
                            before = t[0:np_, g.b, k - 1, P - 1:P] if k else t[0:np_, 1 - g.b, 3, P - 1:P]
                            v.scalar_tensor_tensor(t[0:np_, g.b, k, :], cont[0:np_, g.b, k, :], before,
                                                   ps[0:np_, bk + g.b, k * P:(k + 1) * P], ALU.mult, ALU.add)\
                                .then_inc(carried.sem, 1)
                            n += 1

                def norm(g, y):
                    for k in range(4):
                        i = v.bn_stats(bn[:, 0, k, :], y[:, k, :])
                    i.then_inc(bn_e.sem, 1)
                    bn_count.wait(p, g)
                    for k in range(4):
                        i = v.bn_aggr(mv[:, 0, g.b, k, :], bn[:, 0, k, :])
                    i.then_inc(mv_e.sem, 1)
                    sd_e.wait(dve, p, g)
                    if p != "tgt0":
                        v.reciprocal(rs[:, 0, g.b, :], sd[:, 0, g.b, :]).then_inc(rs_e.sem, 1)
                        rs_e.wait(dve, p, g)
                    (out_scattered if p == "LU" else out_st).wait(dve, p, g, back=2)
                    for k in range(4):
                        i = v.tensor_scalar(outb[:, g.b, k, :], y[:, k, :], mv[:, 0, g.b, k, 0:1], dev(0, g.b, k),
                                            ALU.subtract, ALU.mult)
                    i.then_inc(out_made.sem, 1)

                def stepped(i, g, k):
                    i.then_inc(step.sem, 1)
                    step.wait(dve, p, g, k=k)

                def turn(g):
                    carry(g)
                    select(g.less(-1))
                    if p == "tgt0":
                        first_product.wait(dve, p, g)
                        v.tensor_scalar(hT[:, 1], bank(5), b1_col[:, :], 0.0, ALU.add, ALU.max).then_inc(softplus_in.sem, 1)
                        softplus_in.wait(dve, p, g)
                        softplus.wait(dve, p, g, k=3)
                        product.wait(dve, p, g, back=1)
                        v.tensor_tensor(yTa[:, :, :], hT[:, 0], hT[:, 1], ALU.add).then_inc(softplus_made.sem, 1)
                        product.wait(dve, p, g)
                        stepped(v.scalar_tensor_tensor(y3[:, :, :], bank(6), 0.5, all4(b2h[:, :]), ALU.mult, ALU.add), g, 1)
                        x_gathered.wait(dve, p, g)
                        stepped(v.tensor_tensor(y1[:, g.b], y3[:, :, :], xin[:, g.b], ALU.add), g, 2)
                        norm(g, y1[:, g.b])
                    elif p == "L1":
                        product.wait(dve, p, g)
                        stepped(v.tensor_scalar(tmpv[:, 0, :], ps[:, 6, 0:4], 1.0, None, ALU.max), g, 1)
                        v.reciprocal(tmpv[:, 1, :], tmpv[:, 0, :]).then_inc(step.sem, 1)
                        v.tensor_tensor(y3[:, :, :], bank(5), all4(b1c[:, :]), ALU.add).then_inc(step.sem, 1)
                        step.wait(dve, p, g, k=3)
                        for k in range(4):
                            i = v.scalar_tensor_tensor(y1[:, g.b, k, :], bank(7)[:, k, :], tmpv[:, 1, k:k + 1], y3[:, k, :],
                                                       ALU.mult, ALU.add)
                        stepped(i, g, 4)
                        norm(g, y1[:, g.b])
                    elif p == "L2":
                        product.wait(dve, p, g)
                        stepped(v.scalar_tensor_tensor(y1[:, g.b], bank(5), 0.0, xin[:, g.b], ALU.max, ALU.add), g, 1)
                        norm(g, y1[:, g.b])
                    elif p == "LU":
                        turned.wait(dve, p, g)
                        x_in.wait(dve, p, g)
                        stepped(v.tensor_tensor(y1[:, g.b], bank(4), xin[:, g.b], ALU.add), g, 1)
                        norm(g, y1[:, g.b])
                    else:
                        if p == "T2":
                            product.wait(dve, p, g)
                            stepped(v.tensor_tensor(y3[:, :, :], bank(5), all4(gb2_row[:, :]), ALU.add), g, 1)
                            out_st.wait(dve, p, g, back=2)
                            v.tensor_tensor(outb[:, g.b], y3[:, :, :], xin[:, g.b], ALU.add).then_inc(out_made.sem, 1)
                        if p == "LH":
                            product.wait(dve, p, g)
                            x_in.wait(dve, p, g)
                            out_st.wait(dve, p, g, back=2)
                            v.tensor_tensor(outb[:, g.b], bank(6), xin[:, g.b], ALU.add).then_inc(out_made.sem, 1)

                enter(dve, p)
                v.memset(agg_a[:, 1, 3, P - 1:P], 0.0)
                link(v.memset(agg_b[:, 1, 3, P - 1:P], 0.0))
                select(Turn(None, 0))
                run_turns(dve, p, QUADS, 2, 0, turn, [bn_e_count] if p in bn_e.per else [])
                leave(dve)

            bn_e_count = Count(dve, "bn_e_count", bn_e)
            edge_pass("tgt0")

            bn0_count, bn2_count, bn3_count = (Count(dve, n, s, back) for n, s, back in (
                ("bn0_count", bn0, 0), ("bn2_count", bn2, 1), ("bn3_count", bn3, 4)))

            def stats(n, y, s):
                for k in range(4):
                    i = v.bn_stats(bn[:, n, k, :], y[:, k, :])
                i.then_inc(s.sem, 1)

            def aggregate(n, b, s):
                for k in range(4):
                    i = v.bn_aggr(mv[:, n, b, k, :], bn[:, n, k, :])
                i.then_inc(s.sem, 1)

            def row_pass(p, n):
                nodes = p == "nodes"

                def turn(g):
                    g1, g2, g3, g4 = (g.less(k) for k in (1, 2, 3, 4))
                    i0, i1, i2, i3, i4 = (t.inside(n) for t in (g, g1, g2, g3, g4))
                    i4 = i4 and nodes
                    if i0:
                        y0_made.wait(dve, p, g)
                        stats(0, y0[:, g.b], bn0)
                    if i2:
                        sd2.wait(dve, p, g2)
                        x3_made.wait(dve, p, g2, back=2)
                        v.reciprocal(rs[:, 2, g2.b, :], sd[:, 2, g2.b, :]).then_inc(rs2.sem, 1)
                    if i4:
                        p3_made.wait(dve, p, g4)
                        x3b_made.wait(dve, p, g4)
                        out_made.wait(dve, p, g4, back=1)
                        v.tensor_tensor(y3[:, :, :], bank(7), x3b[:, g4.b], ALU.add).then_inc(y3_made.sem, 1)
                    if i0:
                        bn0_count.wait(p, g)
                        aggregate(0, g.b, mv0)
                    if nodes and i1:
                        look_in.wait(dve, p, g1)
                        v.tensor_scalar(looked[:, bass.ds(g1.lin(1), 1), :].rearrange("p a c -> p (a c)"), lk[:, g1.b, :],
                                        1.0, None, ALU.mult).then_inc(looked_up.sem, 1)
                    if i4:
                        y3_made.wait(dve, p, g4)
                        stats(2, y3, bn3)
                    if i0:
                        sd0.wait(dve, p, g)
                        v.reciprocal(rs[:, 0, g.b, :], sd[:, 0, g.b, :]).then_inc(rs0.sem, 1)
                    if i4:
                        bn3_count.wait(p, g4)
                        aggregate(2, g4.b, mv3)
                    if i0:
                        rs0.wait(dve, p, g)
                        p1_made.wait(dve, p, g)
                        y1_turned.wait(dve, p, g, back=2)
                        squared.wait(dve, p, g, back=2)
                        for k in range(4):
                            i = v.scalar_tensor_tensor(y1[:, g.b, k, :], bank(3)[:, k, :], dev(0, g.b, k), b1c[:, :],
                                                       ALU.mult, ALU.add)
                        i.then_inc(y1_made.sem, 1)
                        if not nodes:
                            out_st.wait(dve, p, g, back=2)
                            for k in range(4):
                                i = v.tensor_scalar(outb[:, g.b, k, :], y0[:, g.b, k, :], mv[:, 0, g.b, k, 0:1],
                                                    dev(0, g.b, k), ALU.subtract, ALU.mult)
                            i.then_inc(x1_made.sem, 1)
                    if i1:
                        p2_made.wait(dve, p, g1)
                        y1_made.wait(dve, p, g1)
                        x3_made.wait(dve, p, g1, back=2)
                        v.scalar_tensor_tensor(u2[:, g1.b], bank(4), 0.0, y1[:, g1.b], ALU.max, ALU.add)\
                            .then_inc(u2_made.sem, 1)
                    if i4:
                        sd3.wait(dve, p, g4)
                        v.reciprocal(rs[:, 3, g4.b, :], sd[:, 3, g4.b, :]).then_inc(rs3.sem, 1)
                    if i1:
                        u2_made.wait(dve, p, g1)
                        stats(1, u2[:, g1.b], bn2)
                    if i4:
                        rs3.wait(dve, p, g4)
                        out_st.wait(dve, p, g4, back=2)
                        for k in range(4):
                            i = v.tensor_scalar(outb[:, g4.b, k, :], y3[:, k, :], mv[:, 2, g4.b, k, 0:1], dev(3, g4.b, k),
                                                ALU.subtract, ALU.mult)
                        i.then_inc(out_made.sem, 1)
                    if i1:
                        bn2_count.wait(p, g1)
                        aggregate(1, g1.b, mv2)
                        mv2.wait(dve, p, g1)
                        v.tensor_scalar(negm[:, g1.b, :], mv[:, 1, g1.b, :, 0], -1.0, None, ALU.mult)
                        squared.wait(dve, p, g1)
                        v.scalar_tensor_tensor(tmpv[:, g1.b, :], ssum[:, g1.b, :], EPS / P, mv[:, 1, g1.b, :, 1],
                                               ALU.mult, ALU.add).then_inc(tv2.sem, 1)
                        if not nodes:
                            sd1.wait(dve, p, g1)
                            v.reciprocal(rs[:, 1, g1.b, :], sd[:, 1, g1.b, :]).then_inc(rs1.sem, 1)
                            rs1.wait(dve, p, g1)
                            more_st.wait(dve, p, g1, back=2)
                            for k in range(4):
                                i = v.tensor_scalar(x3b[:, g1.b, k, :], y1[:, g1.b, k, :], dev(1, g1.b, k), None, ALU.mult)
                            i.then_inc(x2_made.sem, 1)
                    if i3 and not nodes:
                        h_made.wait(dve, p, g3)
                        h_st.wait(dve, p, g3, back=2)
                        v.tensor_tensor(hb[:, g3.b], wide(5), all4(gb1_row[:, :]), ALU.add).then_inc(h_biased.sem, 1)

                enter(dve, p)
                run_turns(dve, p, n, 6, 4, turn, [bn0_count, bn2_count] + ([bn3_count] if nodes else []))

            row_pass("src0", QUADS)
            leave(dve)
            row_pass("nodes", BLOCKS)
            leave(dve)

            enter(dve, "index")
            code, dis_s, dis_d = looked[:, :, 0], looked[:, :, 1], looked[:, :, 3]
            link(v.tensor_tensor(lap_w[:, :], dis_s, dis_d, ALU.mult))
            link(v.scalar_tensor_tensor(lap_w[:, :], lap_w[:, :], -1.0, mask[:, :], ALU.mult, ALU.mult))
            v.tensor_scalar(has, code, float(P), None, ALU.is_ge)
            link(v.tensor_scalar(t_f, code, float(P), -float(P), ALU.max, ALU.add))
            link(v.tensor_copy(s2_i, t_f))
            v.tensor_scalar(t_i, s2_i, 0x7FFFFE00, None, ALU.bitwise_and)
            v.tensor_scalar(nxt_i, s2_i, P - 1, 2, ALU.bitwise_and, ALU.logical_shift_left)
            link(v.tensor_scalar(dst_i, s2_i, 7, 3, ALU.logical_shift_right, ALU.bitwise_and))
            link(v.tensor_tensor(src_f, t_i, nxt_i, ALU.add))
            link(v.tensor_tensor(src_f, src_f, dst_i, ALU.add))
            for r in (rows_of_src, rows_of_lap):
                link(v.tensor_tensor(nxt_f, src_f, r[:, :], ALU.subtract))
                link(v.tensor_tensor(nxt_f, nxt_f, has, ALU.mult))
                link(v.tensor_tensor(r[:, :], nxt_f, r[:, :], ALU.add))
            leave(dve)

            edge_pass("L1", ew_col)
            edge_pass("L2")
            edge_pass("T1", lap_w)
            edge_pass("T2", lap_w)
            edge_pass("LH", lap_w)
            edge_pass("LU", lap_w)

        @block.scalar
        def _(act):
            a = nc.scalar
            act.wait_ge(fixed, 1)
            act.wait_ge(loaded, 16 * LOADS)
            a.activation(sp_col[:, :], b1_col[:, :], ACT.Abs).then_inc(alink, 1)
            act.wait_ge(alink, 1)
            a.activation(sp_col[:, :], sp_col[:, :], ACT.Exp, scale=-1.0).then_inc(alink, 1)
            act.wait_ge(alink, 2)
            a.activation(sp_col[:, :], sp_col[:, :], ACT.Ln, scale=0.5, bias=HALF).then_inc(astep, 1)
            act.wait_ge(roots_in, 1)
            a.activation(flat(x3)[:, 0:BINS], flat(x3)[:, 0:BINS], ACT.Sqrt).then_inc(astep, 1)
            leave(act)

            def keep(p, g, kept, made, free, out_ap, bk):
                made.wait(act, p, g)
                for s, back in free:
                    s.wait(act, p, g, back=back)
                a.activation(out_ap, bank(bk), ACT.Copy).then_inc(kept.sem, 1)

            def root(p, g, s, made, out_ap, in_ap, bias, scale=1.0):
                made.wait(act, p, g)
                a.activation(out_ap, in_ap, ACT.Sqrt, scale=scale, bias=bias).then_inc(s.sem, 1)

            def edge_pass(p):
                def turn(g):
                    if p == "tgt0":
                        softplus_in.wait(act, p, g)
                        softplus_made.wait(act, p, g, back=1)
                        a.activation(hT[:, 0], bank(5), ACT.Abs, bias=b1_col[:, :]).then_inc(softplus.sem, 1)
                        softplus.wait(act, p, g, k=1)
                        a.activation(hT[:, 0], hT[:, 0], ACT.Exp, scale=-1.0).then_inc(softplus.sem, 1)
                        softplus.wait(act, p, g, k=2)
                        a.activation(hT[:, 0], hT[:, 0], ACT.Ln, scale=0.5, bias=HALF).then_inc(softplus.sem, 1)
                        mv_e.wait(act, p, g)
                        a.activation(sd[:, 0, g.b, :], mv[:, 0, g.b, :, 1], ACT.Ln, bias=EPS4).then_inc(softplus.sem, 1)
                        softplus.wait(act, p, g, k=4)
                        out_made.wait(act, p, g, back=2)
                        a.activation(rs[:, 0, g.b, :], sd[:, 0, g.b, :], ACT.Exp, scale=-0.5).then_inc(sd_e.sem, 1)
                        return
                    if p in ("L1", "L2"):
                        keep(p, g, turned_kept, turned, [(product, 1)], yTa[:, :, :], 4)
                    if p == "T2":
                        keep(p, g, turned_kept, turned, [(first_product, 1)], yTa[:, :, :], 4)
                        first_product.wait(act, p, g)
                        product.wait(act, p, g, back=1)
                        h_turned.wait(act, p, g, back=1)
                        for j in range(2):
                            a.activation(hT[:, j], bank(6 + j), ACT.Relu, bias=gb1_col[:, j:j + 1]).then_inc(hidden.sem, 1)
                        h_turned.wait(act, p, g)
                        more_st.wait(act, p, g, back=2)
                        a.activation(hb[:, g.b], wide(2), ACT.Copy).then_inc(h_kept.sem, 1)
                    if p == "T1":
                        turned.wait(act, p, g)
                        out_st.wait(act, p, g, back=2)
                        a.activation(outb[:, g.b], bank(4), ACT.Copy).then_inc(turned_kept.sem, 1)
                    if p == "LH":
                        product.wait(act, p, g)
                        more_st.wait(act, p, g, back=2)
                        a.activation(y1[:, g.b], bank(7), ACT.Copy).then_inc(u_kept.sem, 1)
                    if p in sd_e.per:
                        root(p, g, sd_e, mv_e, sd[:, 0, g.b, :], mv[:, 0, g.b, :, 1], EPS1)

                enter(act, p)
                run_turns(act, p, QUADS, 2, 0, turn)
                leave(act)

            edge_pass("tgt0")

            def row_pass(p, n):
                nodes = p == "nodes"

                def turn(g):
                    g1, g3, g4 = (g.less(k) for k in (1, 3, 4))
                    if g.inside(n):
                        keep(p, g, y0T_kept, y0_turned, [(p1_made, 1)], yTa[:, :, :], 0)
                    if g1.inside(n):
                        keep(p, g1, y1T_kept, y1_turned, [(p2_made, 1)], yTb[:, :, :], 1)
                    if g3.inside(n):
                        keep(p, g3, x3T_kept, x3_turned, [(h_made, 1)], yTc[:, :, :], 2)
                    if g.inside(n):
                        root(p, g, sd0, mv0, sd[:, 0, g.b, :], mv[:, 0, g.b, :, 1], EPS4)
                    if g1.inside(n):
                        y1_made.wait(act, p, g1)
                        tv2.wait(act, p, g1, back=2)
                        squared.wait(act, p, g1, back=1)
                        for k in range(4):
                            i = a.activation(unused[:, k, :], y1[:, g1.b, k, :], ACT.Square, accum_out=ssum[:, g1.b, k:k + 1])
                        i.then_inc(squared.sem, 1)
                        if not nodes:
                            squared.wait(act, p, g1)
                            a.activation(sd[:, 1, g1.b, :], ssum[:, g1.b, :], ACT.Sqrt, scale=1.0 / P, bias=EPS1)\
                                .then_inc(sd1.sem, 1)
                    if nodes and g4.inside(n):
                        root(p, g4, sd3, mv3, sd[:, 3, g4.b, :], mv[:, 2, g4.b, :, 1], EPS1)
                    if g3.inside(n):
                        if nodes:
                            h_made.wait(act, p, g3)
                            p3_made.wait(act, p, g3, back=1)
                            for j in range(2):
                                a.activation(hT[:, j], bank(5 + j), ACT.Relu, bias=gb1_col[:, j:j + 1])\
                                    .then_inc(hidden.sem, 1)
                        else:
                            h_biased.wait(act, p, g3)
                            a.activation(hb[:, g3.b], hb[:, g3.b], ACT.Relu).then_inc(h_kept.sem, 1)
                    if g1.inside(n):
                        root(p, g1, sd2, tv2, sd[:, 2, g1.b, :], tmpv[:, g1.b, :], EPS2)

                enter(act, p)
                run_turns(act, p, n, 6, 4, turn)
                leave(act)

            row_pass("src0", QUADS)
            row_pass("nodes", BLOCKS)
            skip(act, "index")
            for p in ("L1", "L2", "T1", "T2", "LH", "LU"):
                edge_pass(p)

        @block.tensor
        def _(pe):
            t = nc.tensor
            pe.wait_ge(fixed, 1)
            pe.wait_ge(loaded, 16 * LOADS)

            def count_tile(g):
                first, last = (g.reg is None and g.c == c for c in (0, TILES - 1))
                pe.wait_ge(hots, g.lin(1, 1))
                (bin_s, bin_d), (lane_s, lane_t, lane_l) = hot_bin[g.b], hot_lane[g.b]
                for bk, lanes, bins in ((0, lane_s, bin_s), (2, lane_t, bin_d), (4, lane_l, bin_d)):
                    for j, (lo, n) in enumerate(((0, 512), (512, BINS - 512))):
                        i = t.matmul(ps[:, bk + j, 0:n], lanes, bins[:, lo:lo + n], start=first, stop=last)
                i.then_inc(counted, 1)

            pe.wait_ge(vstep, V_COLS)
            run_turns(pe, "", TILES, 2, 0, count_tile)
            t.drain().then_inc(tstep, 1)
            t.transpose(bank(6)[:, 0, :], raw_W1[:, 0:P], ident[:, :])
            t.transpose(ps[0:32, 6, P:2 * P], raw_W1[:, P:ATTR], ident[:, :])
            t.transpose(bank(6)[:, 2, :], raw_W2, ident[:, :])
            t.transpose(bank(6)[:, 3, :], raw_Ws, ident[:, :]).then_inc(tstep, 1)
            pe.wait_ge(vstep, V_WEIGHTS)
            t.matmul(bank(7)[:, 0, :], Bm, center[:, :], start=True, stop=True)
            t.matmul(bank(7)[:, 1, :], raw_Wn, half_center[:, :], start=True, stop=True)
            t.matmul(bank(7)[:, 2, :], bcol, half_center[:, :], start=True, stop=True)
            t.matmul(bank(7)[:, 3, :], spb, W2T[:, :], start=True, stop=True).then_inc(tstep, 1)
            pe.wait_ge(vstep, V_BTC)
            t.matmul(bank(6)[:, 0, :], BtC, center[:, :], start=True, stop=True).then_inc(tstep, 1)
            leave(pe)

            def turn4(p, g, s, source, bk):
                for k in range(4):
                    i = t.transpose(bank(bk)[:, k, :], source[:, k, :], ident[:, :])
                i.then_inc(s.sem, 1)

            def edge_pass(p):
                def sums(g):
                    if not g.inside(QUADS):
                        return
                    (attr_in if p == "tgt0" else rows_in).wait(pe, p, g)
                    if p == "tgt0" and g.reg is None and g.c == QUADS - 1:
                        pe.wait_ge(zeroed, 1)
                        pe.wait_ge(tail_in, 16)
                    selected.wait(pe, p, g)
                    carried.wait(pe, p, g, back=2)
                    for k in range(4):
                        i = t.matmul(bank(g.b)[:, k, :], rows[:, g.b, k, 0:P], sel[:, g.b, k, :], start=True, stop=True)
                        if p == "tgt0":
                            i = t.matmul(ps[0:32, 2 + g.b, k * P:(k + 1) * P], rows[:, g.b, k, P:ATTR], sel[:, g.b, k, :],
                                         start=True, stop=True)
                        if p == "LH":
                            i = t.matmul(bank(2 + g.b)[:, k, :], rows[:, g.b, k, P:HID], sel[:, g.b, k, :],
                                         start=True, stop=True)
                    if p == "L1":
                        i = t.matmul(ps[:, 2 + g.b, :], ones[:, :], sel[:, g.b].rearrange("p k d -> p (k d)"),
                                     start=True, stop=True)
                    i.then_inc(summed.sem, 1)

                def turn(g):
                    q = [agg_a[:, g.b, k, :] for k in range(4)]
                    if p in ("L1", "L2", "T2"):
                        x_in.wait(pe, p, g)
                        turned_kept.wait(pe, p, g, back=1)
                        turn4(p, g, turned, xin[:, g.b], 4)
                    sums(g.less(-1))
                    carried.wait(pe, p, g)
                    if p == "tgt0":
                        softplus.wait(pe, p, g, back=1, k=1)
                        t.matmul(ps[:, 5, :], W1Ta[:, :], agg_a[:, g.b].rearrange("p k d -> p (k d)"), start=True, stop=False)
                        t.matmul(ps[:, 5, :], W1Tb[:, :], agg_b[0:32, g.b].rearrange("p k d -> p (k d)"),
                                 start=False, stop=True).then_inc(first_product.sem, 1)
                        softplus_made.wait(pe, p, g)
                        step.wait(pe, p, g, back=1, k=1)
                        for k in range(4):
                            i = t.matmul(bank(6)[:, k, :], yTa[:, k, :], W2T[:, :], start=True, stop=True)
                        i.then_inc(product.sem, 1)
                    if p == "L1":
                        turned_kept.wait(pe, p, g)
                        step.wait(pe, p, g, back=1, k=4)
                        for k in range(4):
                            t.matmul(ps[:, 6, k:k + 1], agg_b[0:1, g.b, k, :], ones[0:1, 0:1], start=True, stop=True)
                        for k in range(4):
                            t.matmul(bank(5)[:, k, :], yTa[:, k, :], A1[:, :], start=True, stop=True)
                            i = t.matmul(bank(7)[:, k, :], q[k], wn_c[:, :], start=True, stop=True)
                        i.then_inc(product.sem, 1)
                    if p == "L2":
                        turned_kept.wait(pe, p, g)
                        step.wait(pe, p, g, back=1, k=1)
                        for k in range(4):
                            t.matmul(bank(5)[:, k, :], yTa[:, k, :], ws_sb[:, :], start=True, stop=False)
                            i = t.matmul(bank(5)[:, k, :], q[k], wn_sb[:, :], start=False, stop=True)
                        i.then_inc(product.sem, 1)
                    if p == "T1":
                        turned_kept.wait(pe, p, g, back=1)
                        turn4(p, g, turned, agg_a[:, g.b], 4)
                    if p == "LU":
                        step.wait(pe, p, g, back=1, k=1)
                        turn4(p, g, turned, agg_a[:, g.b], 4)
                    if p == "T2":
                        turned_kept.wait(pe, p, g)
                        lap_arrived.wait(pe, p, g)
                        hidden.wait(pe, p, g, back=1)
                        terms = ((G02, yTa[:, :, :]), (Gm1, lap_in[:, g.b]), (G2x2, agg_a[:, g.b]))
                        for j in range(2):
                            for n, (w, r) in enumerate(terms):
                                i = t.matmul(ps[:, 6 + j, :], w[:, j * P:(j + 1) * P], r.rearrange("p k d -> p (k d)"),
                                             start=n == 0, stop=n == 2)
                        i.then_inc(first_product.sem, 1)
                        hidden.wait(pe, p, g)
                        step.wait(pe, p, g, back=1, k=1)
                        for k in range(4):
                            for j in range(2):
                                i = t.matmul(bank(5)[:, k, :], hT[:, j, k, :], V02[:, j, :], start=j == 0, stop=j == 1)
                        i.then_inc(product.sem, 1)
                        h_kept.wait(pe, p, g, back=1)
                        for k in range(4):
                            for j in range(2):
                                i = t.transpose(wide(2)[:, k, j * P:(j + 1) * P], hT[:, j, k, :], ident[:, :])
                        i.then_inc(h_turned.sem, 1)
                    if p == "LH":
                        out_made.wait(pe, p, g, back=1)
                        u_kept.wait(pe, p, g, back=1)
                        for k in range(4):
                            for j in range(2):
                                w = V12[:, :, j * P:(j + 1) * P]
                                t.matmul(bank(6 + j)[:, k, :], q[k], w[:, 0, :], start=True, stop=False)
                                i = t.matmul(bank(6 + j)[:, k, :], agg_b[:, g.b, k, :], w[:, 1, :], start=False, stop=True)
                        i.then_inc(product.sem, 1)

                enter(pe, p)
                sums(Turn(None, 0))
                run_turns(pe, p, QUADS, 2, 0, turn, last=3)
                leave(pe)

            edge_pass("tgt0")

            def row_pass(p, n):
                nodes = p == "nodes"

                def turn(g):
                    g1, g3, g4 = (g.less(k) for k in (1, 3, 4))
                    if g.inside(n):
                        y0_made.wait(pe, p, g)
                        y0T_kept.wait(pe, p, g, back=1)
                        turn4(p, g, y0_turned, y0[:, g.b], 0)
                    if g1.inside(n):
                        y1_made.wait(pe, p, g1)
                        y1T_kept.wait(pe, p, g1, back=1)
                        turn4(p, g1, y1_turned, y1[:, g1.b], 1)
                    if g3.inside(n):
                        x3_made.wait(pe, p, g3)
                        x3T_kept.wait(pe, p, g3, back=1)
                        turn4(p, g3, x3_turned, x3[:, g3.b], 2)
                    if nodes and g4.inside(n):
                        hidden.wait(pe, p, g4)
                        y3_made.wait(pe, p, g4, back=1)
                        for k in range(4):
                            for j in range(2):
                                i = t.matmul(bank(7)[:, k, :], hT[:, j, k, :], V02[:, j, :], start=j == 0, stop=j == 1)
                        i.then_inc(p3_made.sem, 1)
                    if g.inside(n):
                        y0T_kept.wait(pe, p, g)
                        y1_made.wait(pe, p, g, back=1)
                        for k in range(4):
                            i = t.matmul(bank(3)[:, k, :], yTa[:, k, :], A1[:, :], start=True, stop=True)
                        i.then_inc(p1_made.sem, 1)
                    if g1.inside(n):
                        y1T_kept.wait(pe, p, g1)
                        u2_made.wait(pe, p, g1, back=1)
                        for k in range(4):
                            i = t.matmul(bank(4)[:, k, :], yTb[:, k, :], ws_sb[:, :], start=True, stop=True)
                        i.then_inc(p2_made.sem, 1)
                    if g3.inside(n):
                        x3T_kept.wait(pe, p, g3)
                        if nodes:
                            hidden.wait(pe, p, g3, back=1)
                            for j in range(2):
                                i = t.matmul(ps[:, 5 + j, :], G02[:, j * P:(j + 1) * P], yTc[:].rearrange("p k d -> p (k d)"),
                                             start=True, stop=True)
                        else:
                            h_biased.wait(pe, p, g3, back=1)
                            for k in range(4):
                                i = t.matmul(wide(5)[:, k, :], yTc[:, k, :], G02[:, :], start=True, stop=True)
                        i.then_inc(h_made.sem, 1)

                enter(pe, p)
                run_turns(pe, p, n, 6, 4, turn)
                leave(pe)

            row_pass("src0", QUADS)
            row_pass("nodes", BLOCKS)
            skip(pe, "index")
            for p in ("L1", "L2", "T1", "T2", "LH", "LU"):
                edge_pass(p)


_INS = ["x", "src", "dst", "edge_attr3_10x16", "edge_weight", "L0_gnn_W1", "L0_gnn_b1", "L0_gnn_W2", "L0_gnn_b2",
        "L1_gnn_W_self", "L1_gnn_b_self", "L1_gnn_W_neigh", "L1_gnn_b_neigh", "L2_gnn_w_s", "L2_gnn_w_n",
        "L3_gnn_W1", "L3_gnn_b1", "L3_gnn_W2", "L3_gnn_b2"]


def kernel(**inputs):
    import numpy as _np
    import concourse.bacc as _bacc
    from concourse import mybir as _mybir
    from concourse.bass_utils import run_bass_kernel_spmd as _run

    nc = _bacc.Bacc("TRN2", target_bir_lowering=False, num_devices=1)
    arrays, args = {}, []
    for name in _INS:
        a = _np.ascontiguousarray(inputs[name])
        if name == "edge_attr3_10x16":
            a = a.reshape(EDGES, ATTR)
        arrays[f"in_{name}_dram"] = a
        args.append(nc.dram_tensor(f"in_{name}_dram", a.shape, _mybir.dt.from_np(a.dtype), kind="ExternalInput").ap())
    args.append(nc.dram_tensor("out_0_dram", (NODES, P), _mybir.dt.float32, kind="ExternalOutput").ap())
    gnn_kernel(nc, *args)
    r = _run(nc, [arrays], core_ids=[0])
    return r.results[0]["out_0_dram"]
```

```python
from contextlib import ExitStack

import concourse.bass as bass
from concourse import mybir

F32 = mybir.dt.float32
F16 = mybir.dt.float16
I32 = mybir.dt.int32
ALU = mybir.AluOpType
ACT = mybir.ActivationFunctionType

P = 128
NODES = 100000
EDGES = 25000
ATTR = 160
HID = 256
TILES = -(-EDGES // P)
QUADS = TILES // 4
SLOTS = TILES * P
FULL = EDGES // P
REST = EDGES - FULL * P
BLOCKS = -(-NODES // 512)
LAST_BLOCK = NODES - 512
PAD = 1 << 20
BINS = -(-NODES // P)
EPS = 1e-5
assert TILES == 4 * QUADS and QUADS % 2 == 1 and BLOCKS % 2 == 0


class Turn:

    def __init__(self, reg, c):
        self.reg, self.c, self.b = reg, c, c & 1

    def less(self, k):
        return Turn(self.reg, self.c - k)

    def lin(self, scale, add=0):
        if self.reg is None:
            return scale * self.c + add
        r, k = (self.reg if scale == 1 else self.reg * scale), scale * self.c + add
        return r + k if k else r

    def inside(self, n):
        return self.reg is not None or 0 <= self.c < n


class Signal:

    def __init__(self, sem, per, turns):
        self.sem, self.per, self.start, at = sem, per, {}, 0
        for p, n in per.items():
            self.start[p] = at
            at += turns[p] * n

    def value(self, p, g, back=0, k=None):
        return g.less(back).lin(self.per[p], self.start[p] + (self.per[p] if k is None else k))

    def wait(self, eng, p, g, back=0, k=None):
        if g.reg is not None or g.c >= back:
            eng.wait_ge(self.sem, self.value(p, g, back, k))


class Transfer:

    def __init__(self, sems, n, turns):
        self.sems, self.n, self.start, self.end, at = sems, n, {}, {}, [0, 0]
        for p in n:
            self.start[p] = tuple(at)
            at = [at[b] + 16 * n[p] * ((turns[p] + 1 - b) // 2) for b in range(2)]
            self.end[p] = tuple(at)

    def wait(self, eng, p, g, back=0):
        if g.reg is not None or g.c >= back:
            g, n = g.less(back), self.n[p]
            eng.wait_ge(self.sems[g.b], g.lin(8 * n, self.start[p][g.b] + 16 * n - 8 * n * g.b))

    def wait_all(self, eng, p):
        for b in range(2):
            eng.wait_ge(self.sems[b], self.end[p][b])


class Count:

    def __init__(self, eng, name, what, behind=0):
        self.eng, self.reg, self.what, self.behind = eng, eng.alloc_register(name), what, behind

    def begin(self, p, g):
        self.eng.reg_mov(self.reg, self.what.value(p, g, self.behind))

    def wait(self, p, g):
        if g.reg is None:
            self.what.wait(self.eng, p, g)
        else:
            self.eng.wait_ge(self.what.sem, self.reg)
            self.eng.reg_add(self.reg, self.reg, self.what.per[p])


def run_turns(eng, p, n, lead, tail, body, counts=(), last=1):
    end = (n - last) // 2 * 2
    for c in range(lead):
        body(Turn(None, c))
    for count in counts:
        count.begin(p, Turn(None, lead))
    with eng.Fori(lead, end - 1, 2) as i:
        body(Turn(i, 0))
        body(Turn(i, 1))
    for c in range(end, n + tail):
        body(Turn(None, c))


def gnn_kernel(nc, x, src, dst, attr, ew, W1, b1, W2, b2, Wself, bself, Wneigh, bneigh, ws, wn, G1, gb1, G2, gb2, out):
    ctx = ExitStack()
    with ctx:
        def sb(name, shape, dt=F32):
            return ctx.enter_context(nc.sbuf_tensor(name, shape, dt))

        def sem(name):
            return ctx.enter_context(nc.semaphore(name))

        def dram(name, shape):
            return nc.dram_tensor(name, shape, F32).ap()

        state1, state2, state3 = (dram(f"state{n}", (2 * SLOTS, P)) for n in (1, 2, 3))
        state_h = dram("state_h", (2 * SLOTS, HID))
        lap1, lap2 = dram("lap1", (SLOTS + P, P)), dram("lap2", (SLOTS + P, P))
        lap1_cols = dram("lap1_cols", (QUADS, P, 512))
        near_out, most_out = dram("near_out", (SLOTS, P)), dram("most_out", (SLOTS, P))
        node_table = dram("node_table", (P * BINS, 2))

        def one(v, g):
            return v[g.c] if g.reg is None else v[bass.ds(g.lin(1), 1)].rearrange("a p k d -> (a p) k d")

        def quad_of(t, g, half=0):
            return one(t[half * SLOTS:(half + 1) * SLOTS, :].rearrange("(q p k) d -> q p k d", p=P, k=4), g)

        def block_of(t, g):
            if g.reg is None and g.c == BLOCKS - 1:
                return t[LAST_BLOCK:NODES, :].rearrange("(p k) d -> p k d", k=4)
            return one(t[0:(BLOCKS - 1) * 512, :].rearrange("(q p k) d -> q p k d", p=P, k=4), g)

        dst_row = sb("dst_row", [P, 1 + SLOTS], I32)
        dst_col, ew_col, lap_w, mask = (sb(n, [P, TILES]) for n in ("dst_col", "ew_col", "lap_w", "mask"))
        src_g, dst_g, rows_of_src, rows_of_lap, out_row = (
            sb(n, [P, TILES], I32) for n in ("src_g", "dst_g", "rows_of_src", "rows_of_lap", "out_row"))
        look_idx = sb("look_idx", [P, TILES, 2], I32)
        looked = sb("looked", [P, TILES, 4])
        zero_i = sb("zero_i", [P, 4], I32)
        ident, center, half_center, ones, A1, wn_c, ws_sb, wn_sb, W1Ta, W2T = (
            sb(n, [P, P]) for n in ("ident", "center", "half_center", "ones", "A1", "wn_c", "ws_sb", "wn_sb", "W1Ta", "W2T"))
        W1Tb = sb("W1Tb", [32, P])
        G02, Gm1, G2x2 = (sb(n, [P, HID]) for n in ("G02", "Gm1", "G2x2"))
        V02 = sb("V02", [P, 2, P])
        V12 = sb("V12", [P, 2, HID])
        c0h, b1c, b2h, gb2_row = (sb(n, [P, P]) for n in ("c0h", "b1c", "b2h", "gb2_row"))
        gb1_row = sb("gb1_row", [P, HID])
        gb1_col = sb("gb1_col", [P, 2])
        b1_col, bs_col, bn_col, sp_col = (sb(n, [P, 1]) for n in ("b1_col", "bs_col", "bn_col", "sp_col"))
        consts = sb("consts", [P, 4])
        EPS4, EPS1, EPS2, HALF = (consts[:, n:n + 1] for n in range(4))

        xin, y0, y1, u2, x3, x3b, outb = (sb(n, [P, 2, 4, P]) for n in ("xin", "y0", "y1", "u2", "x3", "x3b", "outb"))
        yTa, yTb, yTc = (sb(n, [P, 4, P]) for n in ("yTa", "yTb", "yTc"))
        y3 = sb("y3", [P, 2, 4, P])
        hT = sb("hT", [P, 2, 4, P])
        rows, hb = (sb(n, [P, 2, 4, HID]) for n in ("rows", "hb"))
        cont = sb("cont", [P, 2, 4, P], F16)
        zeros = sb("zeros", [P, P])
        unused = sb("unused", [P, 4, P], mybir.dt.bfloat16)
        ssum, tmpv, negm, off3 = (sb(n, [P, 2, 4]) for n in ("ssum", "tmpv", "negm", "off3"))
        bn = sb("bn", [P, 3, 4, 6])
        mv = sb("mv", [P, 3, 2, 4, 2])
        sd, rs = sb("sd", [P, 4, 2, 4]), sb("rs", [P, 4, 2, 4])
        idx, idx_out = sb("idx", [P, 2, 4], I32), sb("idx_out", [P, 2, 4], I32)
        lk = sb("lk", [P, 2, 4])
        sel, agg_a, agg_b, lap_in = u2, x3, x3b, y0

        ps = ctx.enter_context(nc.psum_tensor("ps", [P, 8, 512], F32))

        def bank(n):
            return ps[:, n, :].rearrange("p (k d) -> p k d", k=4)

        def wide(n):
            return ps[:, n:n + 2, :].rearrange("p n (k d) -> p (n k) d", d=HID)

        def all4(row):
            return row.unsqueeze(1).to_broadcast([P, 4, row.shape[1]])

        turns = {"tgt0": QUADS, "src0": QUADS, "nodes": BLOCKS, "index": 0, "L1": QUADS, "L2": QUADS, "T1": QUADS,
                 "T2": QUADS, "LH": QUADS, "LU": QUADS}
        PASSES = list(turns)
        AGG = ["tgt0", "L1", "L2", "T1", "T2", "LH", "LU"]

        LATE = {"tgt0": 2, "L1": 1, "L2": 1, "T1": 0, "T2": 1, "LH": 1, "LU": 1}

        def signal(name, per):
            per = per if isinstance(per, dict) else {p: 1 for p in per.split()}
            return Signal(sem(name), per, turns)

        def transfer(name, **n):
            return Transfer([sem(name + "_even"), sem(name + "_odd")], n, turns)

        x_gathered = transfer("x_gathered", tgt0=4, src0=4)
        attr_in = transfer("attr_in", tgt0=1)
        out_scattered = transfer("out_scattered", LU=4)
        x_in = transfer("x_in", nodes=1, L1=1, L2=1, T2=1, LH=1, LU=1)
        rows_in = transfer("rows_in", L1=4, L2=4, T1=4, T2=4, LH=4, LU=4)
        tail_in = sem("tail_in")
        look_in = transfer("look_in", nodes=2)
        lap_arrived = transfer("lap_arrived", T2=1)
        out_st = transfer("out_st", tgt0=1, src0=1, nodes=1, L1=1, L2=1, T1=1, T2=1, LH=1)
        more_st = transfer("more_st", src0=1, T1=1, T2=1, LH=1)
        x3_st = transfer("x3_st", src0=1)
        h_st = transfer("h_st", src0=1)
        staged = signal("staged", "tgt0 src0 nodes L1 L2 T1 T2 LH LU")
        out_staged = signal("out_staged", "LU")
        y0_made = signal("y0_made", "src0 nodes")
        x3_made = signal("x3_made", "src0 nodes")
        x3b_made = signal("x3b_made", "nodes")
        bn0, mv0, rs0, y1_made = (signal(n, "src0 nodes") for n in ("bn0", "mv0", "rs0", "y1_made"))
        u2_made, bn2, mv2, tv2, rs2 = (signal(n, "src0 nodes") for n in ("u2_made", "bn2", "mv2", "tv2", "rs2"))
        y3_made, bn3, mv3, rs3, off3_made, looked_up = (
            signal(n, "nodes") for n in ("y3_made", "bn3", "mv3", "rs3", "off3_made", "looked_up"))
        x1_made, rs1, x2_made, h_biased = (signal(n, "src0") for n in ("x1_made", "rs1", "x2_made", "h_biased"))
        selected = signal("selected", {p: 1 for p in AGG})
        carried = signal("carried", {p: 8 if p in ("tgt0", "L1", "LH") else 4 for p in AGG})
        step = signal("step", {"tgt0": 2, "L1": 4, "L2": 1, "T2": 1, "LU": 1})
        softplus_in, softplus_made = signal("softplus_in", "tgt0"), signal("softplus_made", "tgt0")
        bn_e, mv_e = signal("bn_e", "tgt0 L1 L2 LU"), signal("mv_e", "tgt0 L1 L2 LU")
        rs_e = signal("rs_e", "L1 L2 LU")
        out_made = signal("out_made", "tgt0 nodes L1 L2 T2 LH LU")
        y0T_kept, sd0, y1T_kept, squared, x3T_kept, sd2 = (
            signal(n, "src0 nodes") for n in ("y0T_kept", "sd0", "y1T_kept", "squared", "x3T_kept", "sd2"))
        sd1, h_kept = signal("sd1", "src0"), signal("h_kept", "src0 T2")
        sd3 = signal("sd3", "nodes")
        hidden = signal("hidden", {"nodes": 2, "T2": 2})
        softplus, ln_e = signal("softplus", {"tgt0": 3}), signal("ln_e", "tgt0")
        sd_e = signal("sd_e", "tgt0 L1 L2 LU")
        turned_kept = signal("turned_kept", "L1 L2 T1 T2")
        u_kept = signal("u_kept", "LH")
        y0_turned, p1_made, y1_turned, p2_made, x3_turned, h_made = (
            signal(n, "src0 nodes") for n in ("y0_turned", "p1_made", "y1_turned", "p2_made", "x3_turned", "h_made"))
        p3_made = signal("p3_made", "nodes")
        summed = signal("summed", {p: 1 for p in AGG})
        turned = signal("turned", "L1 L2 T1 T2 LU")
        first_product = signal("first_product", "tgt0 T2")
        product = signal("product", "tgt0 L1 L2 T2 LH")
        h_turned = signal("h_turned", "T2")
        loaded, pads, zeroed, tables_st, fixed, vstep, tstep, astep, pstep, alink, dlink, roots_in, hots, counted, row_in = (
            sem(n) for n in ("loaded", "pads", "zeroed", "tables_st", "fixed", "vstep", "tstep", "astep", "pstep",
                             "alink", "dlink", "roots_in", "hots", "counted", "row_in"))
        seam = sem("seam")

        def enter(eng, p):
            eng.wait_ge(seam, 5 * (PASSES.index(p) + 1))

        def skip(eng, p):
            enter(eng, p)
            leave(eng)

        def leave(eng):
            eng.drain().then_inc(seam, 1)

        def flat(t):
            return t[:].rearrange("p a k d -> p (a k d)")

        def cols(t, n, dt=F32):
            v = flat(t)[:, n * TILES:(n + 1) * TILES]
            return v if dt == F32 else v.bitcast(dt)

        src_i, dst_i, nxt_i, t_i, s_i = (cols(xin, n, I32) for n in range(5))
        a_src, b_src, a_dst, b_dst, rep = (cols(y0, n) for n in range(5))
        v_tile, v_lane, src_f, nxt_f = (cols(y1, n) for n in range(4))
        s2_i, t_f, has = cols(outb, 0, I32), cols(outb, 1), cols(outb, 2)
        hot = hb[:].rearrange("p a k d -> p (a k d)").bitcast(F16)
        hot_bin = [[hot[:, (2 * b + j) * BINS:(2 * b + j + 1) * BINS] for j in range(2)] for b in range(2)]
        hot_lane = [[hot[:, 4 * BINS + (3 * b + j) * P:4 * BINS + (3 * b + j + 1) * P] for j in range(3)] for b in range(2)]
        iotas = y3[:, 0].rearrange("p k d -> p (k d)").bitcast(F16)
        iota_bin, iota_lane = iotas[:, 0:BINS], iotas[:, BINS:BINS + P]
        table = rows[:].rearrange("p a k d -> p (a k d)")[:, 0:2 * BINS].rearrange("p (n c) -> p n c", c=2)
        raw_G1 = flat(x3)[:, 0:3 * HID].rearrange("p (n d) -> p n d", n=3)
        raw_G2 = flat(x3b)[:, 0:6 * P].rearrange("p (n d) -> p n d", n=6)
        raw = yTa[:].rearrange("p k d -> p (k d)")
        raw_W1, raw_W2, raw_Ws = raw[:, 0:ATTR], raw[:, ATTR:ATTR + P], raw[:, ATTR + P:ATTR + 2 * P]
        raw_Wn, Bm, BtC, bcol = (yTb[:, n, :] for n in range(4))
        spb, = (yTc[:, n, :] for n in range(1))
        LOADS = 23
        V_COLS, V_WEIGHTS, V_BTC, V_TABLE = 1, 2, 3, 4

        block = ctx.enter_context(nc.Block())

        @block.sync
        def _(sp):
            def load(dst_ap, src_ap):
                sp.dma_start(dst_ap, src_ap).then_inc(loaded, 16)

            def row(v):
                return v.rearrange("(a n) -> a n", a=1)

            with nc.allow_non_contiguous_dma("edge lists with an edge per partition; columns of biases"):
                sp.wait_ge(pads, 1)
                for t, s, n in ((src_i, src, EDGES), (dst_i, dst, EDGES), (nxt_i, dst[1:EDGES], EDGES - 1),
                                (ew_col, ew, EDGES)):
                    load(t[:, 0:FULL], s[0:FULL * P].rearrange("(t p) -> p t", p=P))
                    load(t[0:n - FULL * P, FULL:TILES], s[FULL * P:n].rearrange("(p t) -> p t", t=1))
                load(raw_W1, W1)
                load(raw_W2, W2)
                load(raw_Ws, Wself)
                load(raw_Wn, Wneigh)
                load(ws_sb[:, :], ws)
                load(wn_sb[:, :], wn)
                load(raw_G1, G1.rearrange("n p d -> p n d"))
                load(raw_G2, G2.rearrange("n (j p) d -> p (n j) d", p=P))
                for t, s in ((b1_col, b1), (bs_col, bself), (bn_col, bneigh)):
                    load(t[:, :], s.rearrange("(p a) -> p a", a=1))
                load(gb1_col[:, :], gb1.rearrange("(j p) -> p j", p=P))
                load(b2h[:, :], row(b2).to_broadcast([P, P]))
                load(gb2_row[:, :], row(gb2).to_broadcast([P, P]))
                load(gb1_row[:, :], row(gb1).to_broadcast([P, HID]))
                sp.dma_start(dst_row[:, 1:1 + EDGES], row(dst).to_broadcast([P, EDGES])).then_inc(row_in, 16)
            sp.wait_ge(fixed, 1)
            sp.dma_start(lap1[SLOTS:SLOTS + P, :], zeros[:, :]).then_inc(tables_st, 16)
            sp.dma_start(lap2[SLOTS:SLOTS + P, :], zeros[:, :]).then_inc(tables_st, 16)
            sp.wait_ge(vstep, V_TABLE)
            sp.dma_start(node_table.rearrange("(p n) c -> p n c", p=P), table).then_inc(tables_st, 16)
            sp.wait_ge(loaded, 16 * LOADS)
            sp.wait_ge(tables_st, 48)
            leave(sp)

            def edge_pass(p, state=None, half=0, store=None):
                def state_load(g):
                    if state is not None and g.inside(QUADS):
                        if p == "L1":
                            turned.wait(sp, p, g, back=2)
                        if p in ("L2", "LU"):
                            step.wait(sp, p, g, back=2, k=1)
                        if p in ("T2", "LH"):
                            out_made.wait(sp, p, g, back=2)
                        sp.dma_start(xin[:, g.b], quad_of(state, g, half)).then_inc(x_in.sems[g.b], 16)
                        if p == "T2":
                            first_product.wait(sp, p, g, back=2)
                            v = lap1_cols.rearrange("q p (k d) -> q p k d", k=4)
                            sp.dma_start(lap_in[:, g.b], one(v, g)).then_inc(lap_arrived.sems[g.b], 16)

                def turn(g):
                    state_load(g.less(-1))
                    g = g.less(LATE[p])
                    if not g.inside(QUADS):
                        return
                    if p == "T1":
                        carried.wait(sp, p, g)
                        v = lap1_cols.rearrange("q p (k d) -> q p k d", k=4)
                        sp.dma_start(one(v, g), agg_a[:, g.b]).then_inc(more_st.sems[g.b], 16)
                        turned_kept.wait(sp, p, g)
                    elif p != "LU":
                        out_made.wait(sp, p, g)
                    if store is not None:
                        sp.dma_start(quad_of(store, g), outb[:, g.b]).then_inc(out_st.sems[g.b], 16)
                    if p == "T2":
                        h_kept.wait(sp, p, g)
                        sp.dma_start(quad_of(state_h, g), hb[:, g.b]).then_inc(more_st.sems[g.b], 16)
                    if p == "LH":
                        u_kept.wait(sp, p, g)
                        sp.dma_start(quad_of(lap2, g), y1[:, g.b]).then_inc(more_st.sems[g.b], 16)

                enter(sp, p)
                state_load(Turn(None, 0))
                run_turns(sp, p, QUADS, 4, LATE[p], turn, last=3)
                if store is not None:
                    out_st.wait_all(sp, p)
                if p in more_st.n:
                    more_st.wait_all(sp, p)
                leave(sp)

            def attr_load(g):
                if not g.inside(QUADS):
                    return
                summed.wait(sp, "tgt0", g, back=2)
                if g.reg is None and g.c == QUADS - 1:
                    v = attr[(QUADS - 1) * 512:FULL * P, :].rearrange("(k p) d -> p k d", p=P)
                    sp.dma_start(rows[:, g.b, 0:3, 0:ATTR], v).then_inc(attr_in.sems[g.b], 16)
                    sp.wait_ge(zeroed, 1)
                    sp.dma_start(rows[0:REST, g.b, 3, 0:ATTR], attr[FULL * P:EDGES, :]).then_inc(tail_in, 16)
                else:
                    v = attr[0:(QUADS - 1) * 512, :].rearrange("(q k p) d -> q p k d", p=P, k=4)
                    sp.dma_start(rows[:, g.b, :, 0:ATTR], one(v, g)).then_inc(attr_in.sems[g.b], 16)

            def tgt0_turn(g):
                attr_load(g.less(-1))
                g = g.less(LATE["tgt0"])
                if not g.inside(QUADS):
                    return
                out_made.wait(sp, "tgt0", g)
                sp.dma_start(quad_of(state1, g), outb[:, g.b]).then_inc(out_st.sems[g.b], 16)

            enter(sp, "tgt0")
            attr_load(Turn(None, 0))
            run_turns(sp, "tgt0", QUADS, 4, LATE["tgt0"], tgt0_turn, last=3)
            out_st.wait_all(sp, "tgt0")
            leave(sp)

            def src0_turn(g):
                for signal_, g_, t, buf, tr in ((x1_made, g, state1, outb, out_st), (x2_made, g.less(1), state2, x3b, more_st),
                                                (x3_made, g.less(2), state3, x3, x3_st), (h_kept, g.less(4), state_h, hb, h_st)):
                    if g_.inside(QUADS):
                        signal_.wait(sp, "src0", g_)
                        sp.dma_start(quad_of(t, g_, 1), buf[:, g_.b]).then_inc(tr.sems[g_.b], 16)

            enter(sp, "src0")
            run_turns(sp, "src0", QUADS, 8, 4, src0_turn)
            for tr in (out_st, more_st, x3_st, h_st):
                tr.wait_all(sp, "src0")
            leave(sp)

            def x_load(g):
                if g.inside(BLOCKS):
                    y0_made.wait(sp, "nodes", g, back=2)
                    sp.dma_start(xin[:, g.b], block_of(x, g)).then_inc(x_in.sems[g.b], 16)

            def nodes_turn(g):
                x_load(g.less(-2))
                g5 = g.less(5)
                if g5.inside(BLOCKS):
                    out_made.wait(sp, "nodes", g5)
                    if g5.reg is None and g5.c == BLOCKS - 1:
                        out_st.wait(sp, "nodes", g5, back=1)
                    sp.dma_start(block_of(out, g5), outb[:, g5.b]).then_inc(out_st.sems[g5.b], 16)

            enter(sp, "nodes")
            x_load(Turn(None, 0))
            x_load(Turn(None, 1))
            run_turns(sp, "nodes", BLOCKS, 8, 5, nodes_turn, last=3)
            out_st.wait_all(sp, "nodes")
            leave(sp)
            skip(sp, "index")

            edge_pass("L1", state1, store=state2)
            edge_pass("L2", state2, store=state3)
            edge_pass("T1", store=lap1)
            edge_pass("T2", state3, store=near_out)
            edge_pass("LH", near_out, store=most_out)
            edge_pass("LU", most_out)

        @block.gpsimd
        def _(pool):
            gp = nc.gpsimd
            gp.memset(zeros[:, :], 0.0).then_inc(pstep, 1)
            gp.memset(ident[:, :], 0.0)
            gp.memset(zero_i[:, :], 0)
            gp.memset(ones[:, :], 1.0).then_inc(pstep, 1)
            for n, v in enumerate((EPS / 4, EPS, EPS * EPS, 0.5)):
                gp.memset(consts[:, n:n + 1], v)
            pool.wait_ge(pstep, 2)
            gp.affine_select(out=ident[:, :], in_=ident[:, :], compare_op=ALU.not_equal, fill=1.0, base=0,
                             pattern=[[-1, P]], channel_multiplier=1).then_inc(pstep, 1)
            gp.iota(rows_of_src[:, :], pattern=[[512, QUADS], [1, 4]], base=SLOTS, channel_multiplier=4)
            gp.iota(rows_of_lap[:, :], pattern=[[0, TILES]], base=SLOTS, channel_multiplier=1)
            gp.iota(s2_i, pattern=[[1, TILES]], base=1, channel_multiplier=0)
            gp.iota(s_i, pattern=[[0, TILES]], base=0, channel_multiplier=1)
            gp.iota(flat(u2)[:, 0:BINS].bitcast(I32), pattern=[[1, BINS]], base=0, channel_multiplier=0).then_inc(pstep, 1)
            pool.wait_ge(pstep, 4)
            gp.drain().then_inc(fixed, 1)
            leave(pool)

            staged_count = Count(pool, "staged_count", staged)
            rs2_count = Count(pool, "rs2_count", rs2, behind=2)
            out_count = Count(pool, "out_count", out_made)

            def gather(p, g, table_, index, dest, width, sems, waits):
                for s, back in waits:
                    s.wait(pool, p, g, back=back)
                gp.tensor_tensor(idx[:, g.b, :], index[:, bass.ds(g.lin(4), 4)], zero_i[:, :], ALU.add)\
                    .then_inc(staged.sem, 1)
                staged_count.wait(p, g)
                for k in range(4):
                    gp.indirect_dma_start(out=dest[:, g.b, k, 0:width], out_offset=None, in_=table_,
                                          in_offset=bass.IndirectOffsetOnAxis(ap=idx[:, g.b, k:k + 1], axis=0))\
                        .then_inc(sems.sems[g.b], 16)

            enter(pool, "tgt0")
            def tgt0_turn(g):
                if g.reg is None and g.c == QUADS - 1:
                    summed.wait(pool, "tgt0", g, back=2)
                    gp.memset(rows[:, g.b, 3, 0:ATTR], 0.0).then_inc(zeroed, 1)
                gather("tgt0", g, x, dst_g, xin, P, x_gathered, [(step, 2)])

            run_turns(pool, "tgt0", QUADS, 2, 0, tgt0_turn, [staged_count])
            leave(pool)

            def make_y0(p, g):
                (x_in if p == "nodes" else x_gathered).wait(pool, p, g)
                y0_turned.wait(pool, p, g, back=2)
                bn0.wait(pool, p, g, back=2)
                if p == "src0":
                    x1_made.wait(pool, p, g, back=2)
                gp.tensor_tensor(y0[:, g.b], xin[:, g.b], all4(c0h[:, :]), ALU.add).then_inc(y0_made.sem, 1)

            def row_pass(p, n, meanwhile):
                def turn(g):
                    next_, g2, g3 = g.less(-1), g.less(2), g.less(3)
                    if next_.inside(n):
                        make_y0(p, next_)
                    if p == "nodes" and g3.inside(n):
                        x3_made.wait(pool, p, g3)
                        y3_made.wait(pool, p, g3, back=2)
                        gp.tensor_tensor(x3b[:, g3.b], x3[:, g3.b], all4(gb2_row[:, :]), ALU.add).then_inc(x3b_made.sem, 1)
                    meanwhile(g)
                    if g2.inside(n):
                        x3_turned.wait(pool, p, g2, back=2)
                        (x3_st if p == "src0" else x3b_made).wait(pool, p, g2, back=2)
                        rs2_count.wait(p, g2)
                        for k in range(4):
                            i = gp.tensor_scalar(x3[:, g2.b, k, :], u2[:, g2.b, k, :], negm[:, g2.b, k:k + 1],
                                                 rs[:, 2, g2.b, k:k + 1], ALU.add, ALU.mult)
                        i.then_inc(x3_made.sem, 1)
                return turn

            def src_rows(g):
                g = g.less(-3)
                if g.inside(QUADS):
                    gather("src0", g, x, src_g, xin, P, x_gathered, [(y0_made, 2)])

            enter(pool, "src0")
            for c in range(2):
                gather("src0", Turn(None, c), x, src_g, xin, P, x_gathered, [])
            make_y0("src0", Turn(None, 0))
            gather("src0", Turn(None, 2), x, src_g, xin, P, x_gathered, [(y0_made, 2)])
            staged_count.behind = -3
            run_turns(pool, "src0", QUADS, 8, 4, row_pass("src0", QUADS, src_rows), [staged_count, rs2_count], last=3)
            staged_count.behind = 0
            leave(pool)

            def look(g):
                if g.inside(BLOCKS):
                    look_in.wait(pool, "nodes", g, back=2)
                    looked_up.wait(pool, "nodes", g, back=2)
                    gp.tensor_tensor(idx[:, g.b, 0:2], look_idx[:, bass.ds(g.lin(1), 1), :].rearrange("p a c -> p (a c)"),
                                     zero_i[:, 0:2], ALU.add).then_inc(staged.sem, 1)
                    staged_count.wait("nodes", g)
                    for j in range(2):
                        gp.indirect_dma_start(out=lk[:, g.b, 2 * j:2 * j + 2], out_offset=None, in_=node_table,
                                              in_offset=bass.IndirectOffsetOnAxis(ap=idx[:, g.b, j:j + 1], axis=0))\
                            .then_inc(look_in.sems[g.b], 16)

            assert BLOCKS == TILES
            enter(pool, "nodes")
            make_y0("nodes", Turn(None, 0))
            run_turns(pool, "nodes", BLOCKS, 8, 4, row_pass("nodes", BLOCKS, look), [staged_count, rs2_count])
            leave(pool)
            skip(pool, "index")

            def edge_pass(p, table_, index, width=P):
                enter(pool, p)
                run_turns(pool, p, QUADS, 2, 0,
                          lambda g: gather(p, g, table_, index, rows, width, rows_in, [(summed, 2)]), [staged_count])
                leave(pool)

            edge_pass("L1", state1, rows_of_src)
            edge_pass("L2", state2, rows_of_src)
            edge_pass("T1", state3, rows_of_src)
            edge_pass("T2", lap1, rows_of_lap)
            edge_pass("LH", state_h, rows_of_src, HID)

            def last_turn(g):
                if g.less(-1).inside(QUADS):
                    gather("LU", g.less(-1), lap2, rows_of_lap, rows, P, rows_in, [(summed, 2)])
                g = g.less(LATE["LU"])
                if not g.inside(QUADS):
                    return
                out_scattered.wait(pool, "LU", g, back=2)
                gp.tensor_tensor(idx_out[:, g.b, :], out_row[:, bass.ds(g.lin(4), 4)], zero_i[:, :], ALU.add)\
                    .then_inc(out_staged.sem, 1)
                out_staged.wait(pool, "LU", g)
                out_count.wait("LU", g)
                for k in range(4):
                    gp.indirect_dma_start(out=out, in_=outb[:, g.b, k, :], in_offset=None, bounds_check=NODES - 1,
                                          oob_is_err=False,
                                          out_offset=bass.IndirectOffsetOnAxis(ap=idx_out[:, g.b, k:k + 1], axis=0))\
                        .then_inc(out_scattered.sems[g.b], 16)

            enter(pool, "LU")
            gather("LU", Turn(None, 0), lap2, rows_of_lap, rows, P, rows_in, [])
            staged_count.behind = -1
            out_count.behind = LATE["LU"]
            run_turns(pool, "LU", QUADS, 4, LATE["LU"], last_turn, [staged_count, out_count], last=3)
            out_scattered.wait_all(pool, "LU")

        @block.vector
        def _(dve):
            v = nc.vector
            links = [0]

            def link(i):
                links[0] += 1
                i.then_inc(dlink, 1)
                dve.wait_ge(dlink, links[0])

            for t in (src_i, dst_i, nxt_i):
                v.memset(t, PAD)
            v.memset(ew_col[:, :], 0.0)
            v.memset(dst_row[:, 0:1], -1)
            v.memset(dst_row[:, 1 + EDGES:], PAD).then_inc(pads, 1)
            dve.wait_ge(fixed, 1)
            dve.wait_ge(loaded, 16 * LOADS)

            v.tensor_copy(src_f, src_i)
            v.tensor_copy(dst_col[:, :], dst_i)
            v.tensor_copy(nxt_f, nxt_i)
            v.tensor_copy(v_tile, s2_i)
            v.tensor_copy(v_lane, s_i)
            v.tensor_copy(iota_bin, flat(u2)[:, 0:BINS].bitcast(I32))
            link(v.tensor_copy(iota_lane, flat(u2)[:, 0:P].bitcast(I32)))
            v.tensor_tensor(mask[:, :], src_f, dst_col[:, :], ALU.not_equal)
            link(v.tensor_tensor(rep, dst_col[:, :], nxt_f, ALU.not_equal))
            v.tensor_tensor(v_tile, v_tile, rep, ALU.mult)
            v.tensor_tensor(v_lane, v_lane, rep, ALU.mult)
            link(v.tensor_scalar(t_f, rep, -float(PAD), float(PAD), ALU.mult, ALU.add))
            v.tensor_tensor(out_row[:, :], t_f, dst_col[:, :], ALU.add)
            for ids, a, b in ((src_i, a_src, b_src), (dst_i, a_dst, b_dst)):
                v.tensor_scalar(t_i, ids, 7, None, ALU.logical_shift_right)
                link(v.tensor_scalar(s_i, ids, P - 1, None, ALU.bitwise_and))
                v.tensor_copy(a, t_i)
                link(v.tensor_copy(b, s_i))
            v.tensor_scalar(src_g[:, :], src_f, float(NODES - 1), None, ALU.min)
            link(v.tensor_scalar(dst_g[:, :], dst_col[:, :], float(NODES - 1), None, ALU.min))
            for j, ids in enumerate((src_g, dst_g)):
                v.tensor_scalar(t_i, ids[:, :], 7, None, ALU.logical_shift_right)
                link(v.tensor_scalar(s_i, ids[:, :], P - 1, None, ALU.bitwise_and))
                link(v.scalar_tensor_tensor(look_idx[:, :, j], s_i, float(BINS), t_i, ALU.mult, ALU.add))

            v.drain().then_inc(vstep, 1)

            def one_hot(g):
                if g.reg is not None or g.c >= 2:
                    dve.wait_ge(counted, g.lin(1, -1))
                c = bass.ds(g.lin(1), 1)
                (bin_s, bin_d), (lane_s, lane_t, lane_l) = hot_bin[g.b], hot_lane[g.b]
                v.tensor_scalar(bin_s, iota_bin, a_src[:, c], None, ALU.is_equal)
                v.tensor_scalar(bin_d, iota_bin, a_dst[:, c], None, ALU.is_equal)
                v.tensor_scalar(lane_s, iota_lane, b_src[:, c], mask[:, c], ALU.is_equal, ALU.mult)
                v.tensor_scalar(lane_t, iota_lane, b_dst[:, c], v_tile[:, c], ALU.is_equal, ALU.mult)
                v.tensor_scalar(lane_l, iota_lane, b_dst[:, c], v_lane[:, c], ALU.is_equal, ALU.mult)\
                    .then_inc(hots, 1)

            run_turns(dve, "", TILES, 2, 0, one_hot)

            v.tensor_scalar(center[:, :], ident[:, :], 1.0, -1.0 / P, ALU.mult, ALU.add)
            v.tensor_scalar(half_center[:, :], ident[:, :], 0.5, -0.5 / P, ALU.mult, ALU.add)
            v.tensor_tensor(G02[:, :], raw_G1[:, 0, :], raw_G1[:, 2, :], ALU.subtract)
            v.tensor_copy(Gm1[:, :], raw_G1[:, 1, :])
            v.tensor_scalar(G2x2[:, :], raw_G1[:, 2, :], 2.0, None, ALU.mult)
            v.tensor_tensor(V02[:, :, :], raw_G2[:, 0:2, :], raw_G2[:, 4:6, :], ALU.subtract)
            v.tensor_copy(V12[:, :, 0:P], raw_G2[:, 2:4, :])
            v.tensor_scalar(V12[:, :, P:HID], raw_G2[:, 4:6, :], 2.0, None, ALU.mult)
            link(v.tensor_tensor(bs_col[:, :], bs_col[:, :], bn_col[:, :], ALU.add))
            v.tensor_scalar(bcol, ones[:, :], bs_col[:, :], None, ALU.mult)
            v.tensor_scalar(b2h[:, :], b2h[:, :], 0.5, None, ALU.mult)
            dve.wait_ge(astep, 1)
            link(v.scalar_tensor_tensor(sp_col[:, :], b1_col[:, :], 0.0, sp_col[:, :], ALU.max, ALU.add))
            v.tensor_scalar(spb, ones[:, :], sp_col[:, :], None, ALU.mult)
            dve.wait_ge(tstep, 2)
            v.tensor_copy(W1Ta[:, :], bank(6)[:, 0, :])
            v.tensor_copy(W1Tb[:, :], ps[0:32, 6, P:2 * P])
            v.tensor_copy(W2T[:, :], bank(6)[:, 2, :])
            v.scalar_tensor_tensor(Bm, bank(6)[:, 3, :], 0.5, ident[:, :], ALU.mult, ALU.add).then_inc(vstep, 1)
            dve.wait_ge(tstep, 3)
            v.tensor_copy(BtC, bank(7)[:, 0, :]).then_inc(vstep, 1)
            v.tensor_copy(wn_c[:, :], bank(7)[:, 1, :])
            v.tensor_copy(b1c[:, :], bank(7)[:, 2, :])
            link(v.scalar_tensor_tensor(c0h[:, :], bank(7)[:, 3, :], 0.5, b2h[:, :], ALU.mult, ALU.add))
            dve.wait_ge(tstep, 4)
            v.tensor_copy(A1[:, :], bank(6)[:, 0, :])
            for lo, n, bk in ((0, 512, 0), (512, BINS - 512, 1)):
                v.tensor_copy(table[:, lo:lo + n, 1], ps[:, 4 + bk, 0:n])
                v.tensor_scalar(flat(x3)[:, lo:lo + n], ps[:, bk, 0:n], 1.0, None, ALU.max)
                link(v.tensor_scalar(flat(x3b)[:, lo:lo + n], ps[:, bk, 0:n], 1.0, None, ALU.min))
                link(v.scalar_tensor_tensor(table[:, lo:lo + n, 0], ps[:, 2 + bk, 0:n], float(P), table[:, lo:lo + n, 1],
                                            ALU.mult, ALU.add))
            v.drain().then_inc(roots_in, 1)
            dve.wait_ge(astep, 2)
            link(v.reciprocal(flat(x3)[:, 0:BINS], flat(x3)[:, 0:BINS]))
            link(v.tensor_tensor(table[:, :, 1], flat(x3)[:, 0:BINS], flat(x3b)[:, 0:BINS], ALU.mult))
            v.drain().then_inc(vstep, 1)
            leave(dve)

            def dev(n, b, k):
                return rs[:, n, b, k:k + 1]

            def edge_pass(p, weight=None):
                bn_count = bn_e_count
                two = carried.per[p] == 8

                def select(g):
                    if not g.inside(QUADS):
                        return
                    summed.wait(dve, p, g, back=2)
                    carried.wait(dve, p, g, back=2)
                    r4 = dst_row[:, bass.ds(g.lin(512, 1), 512)].rearrange("p (k d) -> p k d", k=4)
                    ends = dst_row[:, bass.ds(g.lin(512), 512)].rearrange("p (k d) -> p k d", k=4)[:, :, 0:1]
                    v.tensor_tensor(cont[:, g.b], r4, ends.to_broadcast([P, 4, P]), ALU.is_equal)
                    if weight is None:
                        own = dst_col[:, bass.ds(g.lin(4), 4)].unsqueeze(2).to_broadcast([P, 4, P])
                        i = v.tensor_tensor(sel[:, g.b], r4, own, ALU.is_equal)
                    for k in range(4 if weight is not None else 0):
                        c = bass.ds(g.lin(4, k), 1)
                        i = v.tensor_scalar(sel[:, g.b, k, :], r4[:, k, :], dst_col[:, c], weight[:, c],
                                            ALU.is_equal, ALU.mult)
                    i.then_inc(selected.sem, 1)

                def carry(g):
                    summed.wait(dve, p, g)
                    if p in ("L1", "L2", "LH"):
                        product.wait(dve, p, g, back=2)
                    elif p in ("T1", "LU"):
                        turned.wait(dve, p, g, back=2)
                    else:
                        first_product.wait(dve, p, g, back=2)
                    if p == "T1":
                        more_st.wait(dve, p, g, back=2)
                    n = 0
                    parts = [(agg_a, 0, P)] + ([(agg_b, 2, 32 if p == "tgt0" else P)] if two else [])
                    for k in range(4):
                        for t, bk, np_ in parts:
                            if n >= len(parts):
                                carried.wait(dve, p, g, k=n - len(parts) + 1)
                            elif g.reg is not None or g.c > 0:
                                carried.wait(dve, p, g, back=1, k=carried.per[p] - len(parts) + n + 1)
                            before = t[0:np_, g.b, k - 1, P - 1:P] if k else t[0:np_, 1 - g.b, 3, P - 1:P]
                            v.scalar_tensor_tensor(t[0:np_, g.b, k, :], cont[0:np_, g.b, k, :], before,
                                                   ps[0:np_, bk + g.b, k * P:(k + 1) * P], ALU.mult, ALU.add)\
                                .then_inc(carried.sem, 1)
                            n += 1

                def moments(g):
                    for k in range(4):
                        i = v.bn_stats(bn[:, 0, k, :], y1[:, g.b, k, :])
                    i.then_inc(bn_e.sem, 1)
                    bn_count.wait(p, g)
                    for k in range(4):
                        i = v.bn_aggr(mv[:, 0, g.b, k, :], bn[:, 0, k, :])
                    i.then_inc(mv_e.sem, 1)

                def norm(g):
                    sd_e.wait(dve, p, g)
                    if p != "tgt0":
                        v.reciprocal(rs[:, 0, g.b, :], sd[:, 0, g.b, :]).then_inc(rs_e.sem, 1)
                        rs_e.wait(dve, p, g)
                    (out_scattered if p == "LU" else out_st).wait(dve, p, g, back=2)
                    for k in range(4):
                        i = v.tensor_scalar(outb[:, g.b, k, :], y1[:, g.b, k, :], mv[:, 0, g.b, k, 0:1], dev(0, g.b, k),
                                            ALU.subtract, ALU.mult)
                    i.then_inc(out_made.sem, 1)

                def stepped(i, g, k):
                    i.then_inc(step.sem, 1)
                    step.wait(dve, p, g, k=k)

                def turn(g):
                    g1 = g.less(1)
                    if p == "tgt0" and g1.inside(QUADS):
                        first_product.wait(dve, p, g1)
                        softplus_made.wait(dve, p, g1, back=1)
                        v.tensor_scalar(hT[:, 1], bank(5), b1_col[:, :], 0.0, ALU.add, ALU.max).then_inc(softplus_in.sem, 1)
                    if g.inside(QUADS):
                        carry(g)
                    if g.less(LATE[p]).inside(QUADS):
                        finish(g.less(LATE[p]))
                    select(g.less(-2))
                    if p == "tgt0" and g1.inside(QUADS):
                        softplus_in.wait(dve, p, g1)
                        softplus.wait(dve, p, g1, k=3)
                        product.wait(dve, p, g1, back=1)
                        v.tensor_tensor(yTa[:, :, :], hT[:, 0], hT[:, 1], ALU.add).then_inc(softplus_made.sem, 1)
                    if bn_e.per.get(p) and g.less(LATE[p]).inside(QUADS):
                        norm(g.less(LATE[p]))

                def finish(g):
                    if p == "tgt0":
                        product.wait(dve, p, g)
                        stepped(v.scalar_tensor_tensor(y3[:, 0], bank(6), 0.5, all4(b2h[:, :]), ALU.mult, ALU.add), g, 1)
                        x_gathered.wait(dve, p, g)
                        stepped(v.tensor_tensor(y1[:, g.b], y3[:, 0], xin[:, g.b], ALU.add), g, 2)
                        moments(g)
                    elif p == "L1":
                        product.wait(dve, p, g)
                        stepped(v.tensor_scalar(tmpv[:, 0, :], ps[:, 6, 0:4], 1.0, None, ALU.max), g, 1)
                        v.reciprocal(tmpv[:, 1, :], tmpv[:, 0, :]).then_inc(step.sem, 1)
                        v.tensor_tensor(y3[:, 0], bank(5), all4(b1c[:, :]), ALU.add).then_inc(step.sem, 1)
                        step.wait(dve, p, g, k=3)
                        for k in range(4):
                            i = v.scalar_tensor_tensor(y1[:, g.b, k, :], bank(7)[:, k, :], tmpv[:, 1, k:k + 1], y3[:, 0, k, :],
                                                       ALU.mult, ALU.add)
                        stepped(i, g, 4)
                        moments(g)
                    elif p == "L2":
                        product.wait(dve, p, g)
                        stepped(v.scalar_tensor_tensor(y1[:, g.b], bank(5), 0.0, xin[:, g.b], ALU.max, ALU.add), g, 1)
                        moments(g)
                    elif p == "LU":
                        turned.wait(dve, p, g)
                        x_in.wait(dve, p, g)
                        stepped(v.tensor_tensor(y1[:, g.b], bank(4), xin[:, g.b], ALU.add), g, 1)
                        moments(g)
                    else:
                        if p == "T2":
                            product.wait(dve, p, g)
                            out_made.wait(dve, p, g, back=1)
                            stepped(v.tensor_tensor(y3[:, 0], bank(5), all4(gb2_row[:, :]), ALU.add), g, 1)
                            out_st.wait(dve, p, g, back=2)
                            v.tensor_tensor(outb[:, g.b], y3[:, 0], xin[:, g.b], ALU.add).then_inc(out_made.sem, 1)
                        if p == "LH":
                            product.wait(dve, p, g)
                            x_in.wait(dve, p, g)
                            out_st.wait(dve, p, g, back=2)
                            v.tensor_tensor(outb[:, g.b], bank(6), xin[:, g.b], ALU.add).then_inc(out_made.sem, 1)

                enter(dve, p)
                v.memset(agg_a[:, 1, 3, P - 1:P], 0.0)
                link(v.memset(agg_b[:, 1, 3, P - 1:P], 0.0))
                select(Turn(None, 0))
                select(Turn(None, 1))
                bn_count.behind = LATE[p]
                run_turns(dve, p, QUADS, 4, LATE[p], turn, [bn_count] if p in bn_e.per else [], last=3)
                leave(dve)

            bn_e_count = Count(dve, "bn_e_count", bn_e)
            dve.wait_ge(row_in, 16)
            edge_pass("tgt0")

            bn0_count, bn2_count, bn3_count = (Count(dve, n, s, back) for n, s, back in (
                ("bn0_count", bn0, 0), ("bn2_count", bn2, 1), ("bn3_count", bn3, 4)))

            def stats(n, y, s):
                for k in range(4):
                    i = v.bn_stats(bn[:, n, k, :], y[:, k, :])
                i.then_inc(s.sem, 1)

            def aggregate(n, b, s):
                for k in range(4):
                    i = v.bn_aggr(mv[:, n, b, k, :], bn[:, n, k, :])
                i.then_inc(s.sem, 1)

            def row_pass(p, n):
                nodes = p == "nodes"

                def turn(g):
                    g1, g2, g3, g4, g5 = (g.less(k) for k in (1, 2, 3, 4, 5))
                    i0, i1, i2, i3 = (t.inside(n) for t in (g, g1, g2, g3))
                    i4, i5 = (nodes and t.inside(n) for t in (g4, g5))
                    if i0:
                        y0_made.wait(dve, p, g)
                        stats(0, y0[:, g.b], bn0)
                    if i5:
                        sd3.wait(dve, p, g5)
                        out_made.wait(dve, p, g5, back=2)
                        v.reciprocal(rs[:, 3, g5.b, :], sd[:, 3, g5.b, :]).then_inc(rs3.sem, 1)
                    if i0:
                        bn0_count.wait(p, g)
                        aggregate(0, g.b, mv0)
                    if i5:
                        rs3.wait(dve, p, g5)
                        v.scalar_tensor_tensor(off3[:, g5.b, :], mv[:, 2, g5.b, :, 0], -1.0, rs[:, 3, g5.b, :],
                                               ALU.mult, ALU.mult).then_inc(off3_made.sem, 1)
                    if i2:
                        sd2.wait(dve, p, g2)
                        x3_made.wait(dve, p, g2, back=2)
                        v.reciprocal(rs[:, 2, g2.b, :], sd[:, 2, g2.b, :]).then_inc(rs2.sem, 1)
                    if nodes and i1:
                        look_in.wait(dve, p, g1)
                        v.tensor_scalar(looked[:, bass.ds(g1.lin(1), 1), :].rearrange("p a c -> p (a c)"), lk[:, g1.b, :],
                                        1.0, None, ALU.mult).then_inc(looked_up.sem, 1)
                    if i0:
                        sd0.wait(dve, p, g)
                        v.reciprocal(rs[:, 0, g.b, :], sd[:, 0, g.b, :]).then_inc(rs0.sem, 1)
                        rs0.wait(dve, p, g)
                        p1_made.wait(dve, p, g)
                        y1_turned.wait(dve, p, g, back=2)
                        squared.wait(dve, p, g, back=2)
                        for k in range(4):
                            i = v.scalar_tensor_tensor(y1[:, g.b, k, :], bank(3)[:, k, :], dev(0, g.b, k), b1c[:, :],
                                                       ALU.mult, ALU.add)
                        i.then_inc(y1_made.sem, 1)
                        if not nodes:
                            out_st.wait(dve, p, g, back=2)
                            for k in range(4):
                                i = v.tensor_scalar(outb[:, g.b, k, :], y0[:, g.b, k, :], mv[:, 0, g.b, k, 0:1],
                                                    dev(0, g.b, k), ALU.subtract, ALU.mult)
                            i.then_inc(x1_made.sem, 1)
                    if i1:
                        p2_made.wait(dve, p, g1)
                        y1_made.wait(dve, p, g1)
                        x3_made.wait(dve, p, g1, back=2)
                        v.scalar_tensor_tensor(u2[:, g1.b], bank(4), 0.0, y1[:, g1.b], ALU.max, ALU.add)\
                            .then_inc(u2_made.sem, 1)
                    if i4:
                        p3_made.wait(dve, p, g4)
                        x3b_made.wait(dve, p, g4)
                        out_made.wait(dve, p, g4, back=2)
                        v.tensor_tensor(y3[:, g4.b], bank(7), x3b[:, g4.b], ALU.add).then_inc(y3_made.sem, 1)
                    if i1:
                        u2_made.wait(dve, p, g1)
                        stats(1, u2[:, g1.b], bn2)
                    if i4:
                        y3_made.wait(dve, p, g4)
                        stats(2, y3[:, g4.b], bn3)
                    if i1:
                        bn2_count.wait(p, g1)
                        aggregate(1, g1.b, mv2)
                    if i4:
                        bn3_count.wait(p, g4)
                        aggregate(2, g4.b, mv3)
                    if i1:
                        mv2.wait(dve, p, g1)
                        v.tensor_scalar(negm[:, g1.b, :], mv[:, 1, g1.b, :, 0], -1.0, None, ALU.mult)
                        squared.wait(dve, p, g1)
                        v.scalar_tensor_tensor(tmpv[:, g1.b, :], ssum[:, g1.b, :], EPS / P, mv[:, 1, g1.b, :, 1],
                                               ALU.mult, ALU.add).then_inc(tv2.sem, 1)
                        if not nodes:
                            sd1.wait(dve, p, g1)
                            v.reciprocal(rs[:, 1, g1.b, :], sd[:, 1, g1.b, :]).then_inc(rs1.sem, 1)
                            rs1.wait(dve, p, g1)
                            more_st.wait(dve, p, g1, back=2)
                            for k in range(4):
                                i = v.tensor_scalar(x3b[:, g1.b, k, :], y1[:, g1.b, k, :], dev(1, g1.b, k), None, ALU.mult)
                            i.then_inc(x2_made.sem, 1)
                    if i3 and not nodes:
                        h_made.wait(dve, p, g3)
                        h_st.wait(dve, p, g3, back=2)
                        v.tensor_tensor(hb[:, g3.b], wide(5), all4(gb1_row[:, :]), ALU.add).then_inc(h_biased.sem, 1)

                enter(dve, p)
                run_turns(dve, p, n, 8, 5, turn, [bn0_count, bn2_count] + ([bn3_count] if nodes else []))

            row_pass("src0", QUADS)
            leave(dve)
            row_pass("nodes", BLOCKS)
            leave(dve)

            enter(dve, "index")
            code, dis_s, dis_d = looked[:, :, 0], looked[:, :, 1], looked[:, :, 3]
            link(v.tensor_tensor(lap_w[:, :], dis_s, dis_d, ALU.mult))
            link(v.scalar_tensor_tensor(lap_w[:, :], lap_w[:, :], -1.0, mask[:, :], ALU.mult, ALU.mult))
            v.tensor_scalar(has, code, float(P), None, ALU.is_ge)
            link(v.tensor_scalar(t_f, code, float(P), -float(P), ALU.max, ALU.add))
            link(v.tensor_copy(s2_i, t_f))
            v.tensor_scalar(t_i, s2_i, 0x7FFFFE00, None, ALU.bitwise_and)
            v.tensor_scalar(nxt_i, s2_i, P - 1, 2, ALU.bitwise_and, ALU.logical_shift_left)
            link(v.tensor_scalar(dst_i, s2_i, 7, 3, ALU.logical_shift_right, ALU.bitwise_and))
            link(v.tensor_tensor(src_f, t_i, nxt_i, ALU.add))
            link(v.tensor_tensor(src_f, src_f, dst_i, ALU.add))
            for r in (rows_of_src, rows_of_lap):
                link(v.tensor_tensor(nxt_f, src_f, r[:, :], ALU.subtract))
                link(v.tensor_tensor(nxt_f, nxt_f, has, ALU.mult))
                link(v.tensor_tensor(r[:, :], nxt_f, r[:, :], ALU.add))
            leave(dve)

            edge_pass("L1", ew_col)
            edge_pass("L2")
            edge_pass("T1", lap_w)
            edge_pass("T2", lap_w)
            edge_pass("LH", lap_w)
            edge_pass("LU", lap_w)

        @block.scalar
        def _(act):
            a = nc.scalar
            act.wait_ge(fixed, 1)
            act.wait_ge(loaded, 16 * LOADS)
            a.activation(sp_col[:, :], b1_col[:, :], ACT.Abs).then_inc(alink, 1)
            act.wait_ge(alink, 1)
            a.activation(sp_col[:, :], sp_col[:, :], ACT.Exp, scale=-1.0).then_inc(alink, 1)
            act.wait_ge(alink, 2)
            a.activation(sp_col[:, :], sp_col[:, :], ACT.Ln, scale=0.5, bias=HALF).then_inc(astep, 1)
            act.wait_ge(roots_in, 1)
            a.activation(flat(x3)[:, 0:BINS], flat(x3)[:, 0:BINS], ACT.Sqrt).then_inc(astep, 1)
            leave(act)

            def keep(p, g, kept, made, free, out_ap, bk):
                made.wait(act, p, g)
                for s, back in free:
                    s.wait(act, p, g, back=back)
                a.activation(out_ap, bank(bk), ACT.Copy).then_inc(kept.sem, 1)

            def root(p, g, s, made, out_ap, in_ap, bias, scale=1.0):
                made.wait(act, p, g)
                a.activation(out_ap, in_ap, ACT.Sqrt, scale=scale, bias=bias).then_inc(s.sem, 1)

            def edge_pass(p):
                def softplus_of(g):
                    softplus_in.wait(act, p, g)
                    softplus_made.wait(act, p, g, back=1)
                    a.activation(hT[:, 0], bank(5), ACT.Abs, bias=b1_col[:, :]).then_inc(softplus.sem, 1)
                    softplus.wait(act, p, g, k=1)
                    a.activation(hT[:, 0], hT[:, 0], ACT.Exp, scale=-1.0).then_inc(softplus.sem, 1)
                    softplus.wait(act, p, g, k=2)
                    a.activation(hT[:, 0], hT[:, 0], ACT.Ln, scale=0.5, bias=HALF).then_inc(softplus.sem, 1)

                def root_of(g):
                    mv_e.wait(act, p, g)
                    a.activation(sd[:, 0, g.b, :], mv[:, 0, g.b, :, 1], ACT.Ln, bias=EPS4).then_inc(ln_e.sem, 1)
                    ln_e.wait(act, p, g)
                    out_made.wait(act, p, g, back=2)
                    a.activation(rs[:, 0, g.b, :], sd[:, 0, g.b, :], ACT.Exp, scale=-0.5).then_inc(sd_e.sem, 1)

                def turn(g):
                    g1, g2 = g.less(1), g.less(2)
                    if p == "tgt0":
                        if g1.inside(QUADS):
                            softplus_of(g1)
                        if g2.inside(QUADS):
                            root_of(g2)
                        return
                    if p == "T2" and g.inside(QUADS):
                        keep(p, g, turned_kept, turned, [(first_product, 1)], yTa[:, :, :], 4)
                    if p == "T2" and g1.inside(QUADS):
                        h_turned.wait(act, p, g1)
                        more_st.wait(act, p, g1, back=2)
                        a.activation(hb[:, g1.b], wide(2), ACT.Copy).then_inc(h_kept.sem, 1)
                    if p == "T2" and g.inside(QUADS):
                        first_product.wait(act, p, g)
                        product.wait(act, p, g, back=1)
                        h_turned.wait(act, p, g, back=1)
                        for j in range(2):
                            a.activation(hT[:, j], bank(6 + j), ACT.Relu, bias=gb1_col[:, j:j + 1]).then_inc(hidden.sem, 1)
                    if g.inside(QUADS):
                        take(g)
                    if p in sd_e.per and g1.inside(QUADS):
                        root(p, g1, sd_e, mv_e, sd[:, 0, g1.b, :], mv[:, 0, g1.b, :, 1], EPS1)

                def take(g):
                    if p in ("L1", "L2"):
                        keep(p, g, turned_kept, turned, [(product, 1)], yTa[:, :, :], 4)
                    if p == "T1":
                        turned.wait(act, p, g)
                        out_st.wait(act, p, g, back=2)
                        a.activation(outb[:, g.b], bank(4), ACT.Copy).then_inc(turned_kept.sem, 1)
                    if p == "LH":
                        product.wait(act, p, g)
                        more_st.wait(act, p, g, back=2)
                        a.activation(y1[:, g.b], bank(7), ACT.Copy).then_inc(u_kept.sem, 1)

                enter(act, p)
                run_turns(act, p, QUADS, 4, LATE[p], turn, last=3)
                leave(act)

            edge_pass("tgt0")

            def row_pass(p, n):
                nodes = p == "nodes"

                def turn(g):
                    g1, g2, g3, g4, g5 = (g.less(k) for k in (1, 2, 3, 4, 5))
                    if g.inside(n):
                        keep(p, g, y0T_kept, y0_turned, [(p1_made, 1)], yTa[:, :, :], 0)
                    if nodes and g5.inside(n):
                        root(p, g5, sd3, mv3, sd[:, 3, g5.b, :], mv[:, 2, g5.b, :, 1], EPS1)
                    if g1.inside(n):
                        keep(p, g1, y1T_kept, y1_turned, [(p2_made, 1)], yTb[:, :, :], 1)
                    if g2.inside(n):
                        root(p, g2, sd2, tv2, sd[:, 2, g2.b, :], tmpv[:, g2.b, :], EPS2)
                    if g3.inside(n):
                        keep(p, g3, x3T_kept, x3_turned, [(h_made, 1)], yTc[:, :, :], 2)
                    if g.inside(n):
                        root(p, g, sd0, mv0, sd[:, 0, g.b, :], mv[:, 0, g.b, :, 1], EPS4)
                    if g1.inside(n):
                        y1_made.wait(act, p, g1)
                        tv2.wait(act, p, g1, back=2)
                        squared.wait(act, p, g1, back=1)
                        for k in range(4):
                            i = a.activation(unused[:, k, :], y1[:, g1.b, k, :], ACT.Square, accum_out=ssum[:, g1.b, k:k + 1])
                        i.then_inc(squared.sem, 1)
                        if not nodes:
                            squared.wait(act, p, g1)
                            a.activation(sd[:, 1, g1.b, :], ssum[:, g1.b, :], ACT.Sqrt, scale=1.0 / P, bias=EPS1)\
                                .then_inc(sd1.sem, 1)
                    if g4.inside(n) and not nodes:
                        h_biased.wait(act, p, g4)
                        a.activation(hb[:, g4.b], hb[:, g4.b], ACT.Relu).then_inc(h_kept.sem, 1)
                    if nodes and g5.inside(n):
                        off3_made.wait(act, p, g5)
                        out_st.wait(act, p, g5, back=2)
                        for k in range(4):
                            i = a.activation(outb[:, g5.b, k, :], y3[:, g5.b, k, :], ACT.Identity,
                                             bias=off3[:, g5.b, k:k + 1], scale=rs[:, 3, g5.b, k:k + 1])
                        i.then_inc(out_made.sem, 1)
                    if g3.inside(n) and nodes:
                        h_made.wait(act, p, g3)
                        p3_made.wait(act, p, g3, back=1)
                        for j in range(2):
                            a.activation(hT[:, j], bank(5 + j), ACT.Relu, bias=gb1_col[:, j:j + 1])\
                                .then_inc(hidden.sem, 1)

                enter(act, p)
                run_turns(act, p, n, 8, 5, turn)
                leave(act)

            row_pass("src0", QUADS)
            row_pass("nodes", BLOCKS)
            skip(act, "index")
            for p in ("L1", "L2", "T1", "T2", "LH", "LU"):
                edge_pass(p)

        @block.tensor
        def _(pe):
            t = nc.tensor
            pe.wait_ge(fixed, 1)
            pe.wait_ge(loaded, 16 * LOADS)

            def count_tile(g):
                first, last = (g.reg is None and g.c == c for c in (0, TILES - 1))
                pe.wait_ge(hots, g.lin(1, 1))
                (bin_s, bin_d), (lane_s, lane_t, lane_l) = hot_bin[g.b], hot_lane[g.b]
                for bk, lanes, bins in ((0, lane_s, bin_s), (2, lane_t, bin_d), (4, lane_l, bin_d)):
                    for j, (lo, n) in enumerate(((0, 512), (512, BINS - 512))):
                        i = t.matmul(ps[:, bk + j, 0:n], lanes, bins[:, lo:lo + n], start=first, stop=last)
                i.then_inc(counted, 1)

            pe.wait_ge(vstep, V_COLS)
            run_turns(pe, "", TILES, 2, 0, count_tile)
            t.drain().then_inc(tstep, 1)
            t.transpose(bank(6)[:, 0, :], raw_W1[:, 0:P], ident[:, :])
            t.transpose(ps[0:32, 6, P:2 * P], raw_W1[:, P:ATTR], ident[:, :])
            t.transpose(bank(6)[:, 2, :], raw_W2, ident[:, :])
            t.transpose(bank(6)[:, 3, :], raw_Ws, ident[:, :]).then_inc(tstep, 1)
            pe.wait_ge(vstep, V_WEIGHTS)
            t.matmul(bank(7)[:, 0, :], Bm, center[:, :], start=True, stop=True)
            t.matmul(bank(7)[:, 1, :], raw_Wn, half_center[:, :], start=True, stop=True)
            t.matmul(bank(7)[:, 2, :], bcol, half_center[:, :], start=True, stop=True)
            t.matmul(bank(7)[:, 3, :], spb, W2T[:, :], start=True, stop=True).then_inc(tstep, 1)
            pe.wait_ge(vstep, V_BTC)
            t.matmul(bank(6)[:, 0, :], BtC, center[:, :], start=True, stop=True).then_inc(tstep, 1)
            leave(pe)

            def turn4(p, g, s, source, bk):
                for k in range(4):
                    i = t.transpose(bank(bk)[:, k, :], source[:, k, :], ident[:, :])
                i.then_inc(s.sem, 1)

            def edge_pass(p):
                def sums(g):
                    if not g.inside(QUADS):
                        return
                    (attr_in if p == "tgt0" else rows_in).wait(pe, p, g)
                    if p == "tgt0" and g.reg is None and g.c == QUADS - 1:
                        pe.wait_ge(zeroed, 1)
                        pe.wait_ge(tail_in, 16)
                    selected.wait(pe, p, g)
                    carried.wait(pe, p, g, back=2)
                    for k in range(4):
                        i = t.matmul(bank(g.b)[:, k, :], rows[:, g.b, k, 0:P], sel[:, g.b, k, :], start=True, stop=True)
                        if p == "tgt0":
                            i = t.matmul(ps[0:32, 2 + g.b, k * P:(k + 1) * P], rows[:, g.b, k, P:ATTR], sel[:, g.b, k, :],
                                         start=True, stop=True)
                        if p == "LH":
                            i = t.matmul(bank(2 + g.b)[:, k, :], rows[:, g.b, k, P:HID], sel[:, g.b, k, :],
                                         start=True, stop=True)
                    if p == "L1":
                        i = t.matmul(ps[:, 2 + g.b, :], ones[:, :], sel[:, g.b].rearrange("p k d -> p (k d)"),
                                     start=True, stop=True)
                    i.then_inc(summed.sem, 1)

                def first(g):
                    q = [agg_a[:, g.b, k, :] for k in range(4)]
                    carried.wait(pe, p, g)
                    if p == "tgt0":
                        softplus.wait(pe, p, g, back=1, k=1)
                        t.matmul(ps[:, 5, :], W1Ta[:, :], agg_a[:, g.b].rearrange("p k d -> p (k d)"), start=True, stop=False)
                        t.matmul(ps[:, 5, :], W1Tb[:, :], agg_b[0:32, g.b].rearrange("p k d -> p (k d)"),
                                 start=False, stop=True).then_inc(first_product.sem, 1)
                    if p == "L1":
                        turned_kept.wait(pe, p, g)
                        step.wait(pe, p, g, back=1, k=4)
                        for k in range(4):
                            t.matmul(ps[:, 6, k:k + 1], agg_b[0:1, g.b, k, :], ones[0:1, 0:1], start=True, stop=True)
                        for k in range(4):
                            t.matmul(bank(5)[:, k, :], yTa[:, k, :], A1[:, :], start=True, stop=True)
                            i = t.matmul(bank(7)[:, k, :], q[k], wn_c[:, :], start=True, stop=True)
                        i.then_inc(product.sem, 1)
                    if p == "L2":
                        turned_kept.wait(pe, p, g)
                        step.wait(pe, p, g, back=1, k=1)
                        for k in range(4):
                            t.matmul(bank(5)[:, k, :], yTa[:, k, :], ws_sb[:, :], start=True, stop=False)
                            i = t.matmul(bank(5)[:, k, :], q[k], wn_sb[:, :], start=False, stop=True)
                        i.then_inc(product.sem, 1)
                    if p == "T1":
                        turned_kept.wait(pe, p, g, back=1)
                        turn4(p, g, turned, agg_a[:, g.b], 4)
                    if p == "LU":
                        step.wait(pe, p, g, back=1, k=1)
                        turn4(p, g, turned, agg_a[:, g.b], 4)
                    if p == "T2":
                        lap_arrived.wait(pe, p, g)
                        hidden.wait(pe, p, g, back=1)
                        turned_kept.wait(pe, p, g)
                        terms = ((Gm1, lap_in[:, g.b]), (G2x2, agg_a[:, g.b]), (G02, yTa[:, :, :]))
                        for j in range(2):
                            for n, (w, r) in enumerate(terms):
                                i = t.matmul(ps[:, 6 + j, :], w[:, j * P:(j + 1) * P], r.rearrange("p k d -> p (k d)"),
                                             start=n == 0, stop=n == 2)
                        i.then_inc(first_product.sem, 1)
                    if p == "LH":
                        out_made.wait(pe, p, g, back=1)
                        u_kept.wait(pe, p, g, back=1)
                        for k in range(4):
                            for j in range(2):
                                w = V12[:, :, j * P:(j + 1) * P]
                                t.matmul(bank(6 + j)[:, k, :], q[k], w[:, 0, :], start=True, stop=False)
                                i = t.matmul(bank(6 + j)[:, k, :], agg_b[:, g.b, k, :], w[:, 1, :], start=False, stop=True)
                        i.then_inc(product.sem, 1)

                def second(g):
                    if p == "tgt0":
                        softplus_made.wait(pe, p, g)
                        step.wait(pe, p, g, back=1, k=1)
                        for k in range(4):
                            i = t.matmul(bank(6)[:, k, :], yTa[:, k, :], W2T[:, :], start=True, stop=True)
                        i.then_inc(product.sem, 1)
                    if p == "T2":
                        hidden.wait(pe, p, g)
                        step.wait(pe, p, g, back=1, k=1)
                        for k in range(4):
                            for j in range(2):
                                i = t.matmul(bank(5)[:, k, :], hT[:, j, k, :], V02[:, j, :], start=j == 0, stop=j == 1)
                        i.then_inc(product.sem, 1)
                        h_kept.wait(pe, p, g, back=1)
                        for k in range(4):
                            for j in range(2):
                                i = t.transpose(wide(2)[:, k, j * P:(j + 1) * P], hT[:, j, k, :], ident[:, :])
                        i.then_inc(h_turned.sem, 1)

                def turn(g):
                    sums(g.less(-1))
                    if p in ("L1", "L2", "T2") and g.inside(QUADS):
                        x_in.wait(pe, p, g)
                        turned_kept.wait(pe, p, g, back=1)
                        turn4(p, g, turned, xin[:, g.b], 4)
                    if p == "T2" and g.less(1).inside(QUADS):
                        second(g.less(1))
                    if g.inside(QUADS):
                        first(g)
                    if p == "tgt0" and g.less(1).inside(QUADS):
                        second(g.less(1))

                enter(pe, p)
                sums(Turn(None, 0))
                run_turns(pe, p, QUADS, 4, 1, turn, last=3)
                leave(pe)

            edge_pass("tgt0")

            def row_pass(p, n):
                nodes = p == "nodes"

                def turn(g):
                    g1, g3, g4 = (g.less(k) for k in (1, 3, 4))
                    if g.inside(n):
                        y0_made.wait(pe, p, g)
                        y0T_kept.wait(pe, p, g, back=1)
                        turn4(p, g, y0_turned, y0[:, g.b], 0)
                    if g1.inside(n):
                        y1_made.wait(pe, p, g1)
                        y1T_kept.wait(pe, p, g1, back=1)
                        turn4(p, g1, y1_turned, y1[:, g1.b], 1)
                    if g3.inside(n):
                        x3_made.wait(pe, p, g3)
                        x3T_kept.wait(pe, p, g3, back=1)
                        turn4(p, g3, x3_turned, x3[:, g3.b], 2)
                    if g.inside(n):
                        y0T_kept.wait(pe, p, g)
                        y1_made.wait(pe, p, g, back=1)
                        for k in range(4):
                            i = t.matmul(bank(3)[:, k, :], yTa[:, k, :], A1[:, :], start=True, stop=True)
                        i.then_inc(p1_made.sem, 1)
                    if g1.inside(n):
                        y1T_kept.wait(pe, p, g1)
                        u2_made.wait(pe, p, g1, back=1)
                        for k in range(4):
                            i = t.matmul(bank(4)[:, k, :], yTb[:, k, :], ws_sb[:, :], start=True, stop=True)
                        i.then_inc(p2_made.sem, 1)
                    if nodes and g4.inside(n):
                        hidden.wait(pe, p, g4)
                        y3_made.wait(pe, p, g4, back=1)
                        for k in range(4):
                            for j in range(2):
                                i = t.matmul(bank(7)[:, k, :], hT[:, j, k, :], V02[:, j, :], start=j == 0, stop=j == 1)
                        i.then_inc(p3_made.sem, 1)
                    if g3.inside(n):
                        x3T_kept.wait(pe, p, g3)
                        if nodes:
                            hidden.wait(pe, p, g3, back=1)
                            for j in range(2):
                                i = t.matmul(ps[:, 5 + j, :], G02[:, j * P:(j + 1) * P], yTc[:].rearrange("p k d -> p (k d)"),
                                             start=True, stop=True)
                        else:
                            h_biased.wait(pe, p, g3, back=1)
                            for k in range(4):
                                i = t.matmul(wide(5)[:, k, :], yTc[:, k, :], G02[:, :], start=True, stop=True)
                        i.then_inc(h_made.sem, 1)

                enter(pe, p)
                run_turns(pe, p, n, 8, 5, turn)
                leave(pe)

            row_pass("src0", QUADS)
            row_pass("nodes", BLOCKS)
            skip(pe, "index")
            for p in ("L1", "L2", "T1", "T2", "LH", "LU"):
                edge_pass(p)


_INS = ["x", "src", "dst", "edge_attr3_10x16", "edge_weight", "L0_gnn_W1", "L0_gnn_b1", "L0_gnn_W2", "L0_gnn_b2",
        "L1_gnn_W_self", "L1_gnn_b_self", "L1_gnn_W_neigh", "L1_gnn_b_neigh", "L2_gnn_w_s", "L2_gnn_w_n",
        "L3_gnn_W1", "L3_gnn_b1", "L3_gnn_W2", "L3_gnn_b2"]


def kernel(**inputs):
    import numpy as _np
    import concourse.bacc as _bacc
    from concourse import mybir as _mybir
    from concourse.bass_utils import run_bass_kernel_spmd as _run

    nc = _bacc.Bacc("TRN2", target_bir_lowering=False, num_devices=1)
    arrays, args = {}, []
    for name in _INS:
        a = _np.ascontiguousarray(inputs[name])
        if name == "edge_attr3_10x16":
            a = a.reshape(EDGES, ATTR)
        arrays[f"in_{name}_dram"] = a
        args.append(nc.dram_tensor(f"in_{name}_dram", a.shape, _mybir.dt.from_np(a.dtype), kind="ExternalInput").ap())
    args.append(nc.dram_tensor("out_0_dram", (NODES, P), _mybir.dt.float32, kind="ExternalOutput").ap())
    gnn_kernel(nc, *args)
    r = _run(nc, [arrays], core_ids=[0])
    return r.results[0]["out_0_dram"]
```
